# Optimizing a Trainium2 kernel written in Bass

```python
import numpy as np
import jax
import jax.numpy as jnp

def _softmax(x, axis=-1):
    return jax.nn.softmax(x, axis=axis)

def _gelu(x):
    return jax.nn.gelu(x, approximate=True)

def _silu(x):
    return jax.nn.silu(x)

def _sigmoid(x):
    return jax.nn.sigmoid(x)

def _layernorm(x, axis=-1, eps=1e-05):
    m = jnp.mean(x, axis=axis, keepdims=True)
    v = jnp.var(x, axis=axis, keepdims=True)
    return (x - m) / jnp.sqrt(v + eps)

def _scatter_add(tgt, idx, src, axis=0):
    return tgt.at[idx].add(src)

def _segment_sum(src, seg, n):
    return jax.ops.segment_sum(src, seg, n)
kernel_name = 'mk_xattn_ffn_d2_seqx_r8_6b820c'

def setup_inputs(seed: int=0):
    np.random.seed(seed)
    _w = jnp.asarray

    def _rec_inputs():
        import jax
        import jax.numpy as jnp
        _rk = jax.random.key(seed)
        x = 0.002226 + 0.9996 * jax.random.normal(jax.random.fold_in(_rk, 1), (8, 128, 128), jnp.float32)
        _lenS = 128 - jax.random.randint(jax.random.fold_in(_rk, 7), (8,), 0, max(1, 128 // 4) + 1, jnp.int32)
        _lenS2 = 128 - jax.random.randint(jax.random.fold_in(_rk, 8), (8,), 0, max(1, 128 // 4) + 1, jnp.int32)
        _ctx_1024P = jax.random.normal(jax.random.fold_in(_rk, 11), (8, 16, 128), jnp.float32)
        _ctx_1024c = jax.random.dirichlet(jax.random.fold_in(_rk, 511), 0.3 * jnp.ones((16,), jnp.float32), (8, 128))
        _ctx_1024t = jnp.einsum('bsk,bkd->bsd', _ctx_1024c, _ctx_1024P)
        _ctx_1024t = _ctx_1024t * jax.lax.rsqrt(jnp.mean(jnp.square(_ctx_1024t)) + 1e-12) * 0.953939
        ctx_1024 = -7.10856e-05 + 0.999911 * (_ctx_1024t + 0.3 * jax.random.normal(jax.random.fold_in(_rk, 611), (8, 128, 128), jnp.float32))
        _validS = jnp.arange(128)[None, :] < _lenS[:, None]
        _validS2 = jnp.arange(128)[None, :] < _lenS2[:, None]
        _causal = jnp.tril(jnp.ones((128, 128), dtype=bool))
        mask_BxS2_bk0 = jnp.logical_not(jnp.broadcast_to(_validS2[:, :], (8, 128)))
        return (x, ctx_1024, mask_BxS2_bk0)
    x, ctx_1024, mask_BxS2_bk0 = _rec_inputs()

    def _L0_xattn_setup():
        import jax, jax.numpy as jnp
        import numpy as np
        DIM, DIM_HEAD, HEADS, SCALE = (128, 64, 8, 8.0)
        INNER = DIM_HEAD * HEADS
        LN_EPS = 1e-05
        L2_EPS = 1e-12

        def layer_norm(x, w, b):
            mu = jnp.mean(x, axis=-1, keepdims=True)
            var = jnp.mean(jnp.square(x - mu), axis=-1, keepdims=True)
            return (x - mu) * jax.lax.rsqrt(var + LN_EPS) * w + b

        def l2norm(t):
            n = jnp.sqrt(jnp.sum(jnp.square(t), axis=-1, keepdims=True))
            return t / jnp.maximum(n, L2_EPS)
        key = jax.random.key(seed)
        ks = jax.random.split(key, 8)
        b, n, m = (8, 1024, 64)
        x = jax.random.normal(ks[0], (b, n, DIM), dtype=jnp.float32)
        latents = jax.random.normal(ks[1], (b, m, DIM), dtype=jnp.float32)
        mask = jax.random.randint(ks[2], (b, n), 0, 2) > 0
        Wq = jax.random.normal(ks[3], (DIM, INNER), dtype=jnp.float32) * DIM ** (-0.5)
        Wkv = jax.random.normal(ks[4], (DIM, 2 * INNER), dtype=jnp.float32) * DIM ** (-0.5)
        Wo = jax.random.normal(ks[5], (INNER, DIM), dtype=jnp.float32) * INNER ** (-0.5)
        return {'x': x, 'latents': latents, 'mask': mask, 'ln_x_w': jnp.ones((DIM,)), 'ln_x_b': jnp.zeros((DIM,)), 'ln_l_w': jnp.ones((DIM,)), 'ln_l_b': jnp.zeros((DIM,)), 'Wq': Wq, 'Wkv': Wkv, 'q_scale': jnp.ones((DIM_HEAD,)), 'k_scale': jnp.ones((DIM_HEAD,)), 'Wo': Wo, 'ln_o_w': jnp.ones((DIM,)), 'ln_o_b': jnp.zeros((DIM,))}
    _L0_xattn_all = _L0_xattn_setup()
    _L0_xattn_in = {k: v for k, v in _L0_xattn_all.items() if k in ('ln_x_w', 'ln_x_b', 'ln_l_w', 'ln_l_b', 'Wq', 'Wkv', 'q_scale', 'k_scale', 'Wo', 'ln_o_w', 'ln_o_b')}
    del _L0_xattn_all

    def _L0_ffn_setup():
        import jax, jax.numpy as jnp
        import numpy as np
        GROUP = 16
        EPS = 1e-05

        def _dequant(q, scale):
            w = q.astype(jnp.float32) / 7.5 - 1.0
            return w * jnp.repeat(scale, GROUP, axis=1)

        def _qlora_linear(x, q, scale, bias, la, lb):
            w = _dequant(q, scale)
            base = jnp.einsum('btd,od->bto', x, w) + bias
            lora = jnp.einsum('btr,or->bto', jnp.einsum('btd,rd->btr', x, la), lb)
            return base + lora

        def _layernorm(x, g, b):
            mu = jnp.mean(x, axis=-1, keepdims=True)
            var = jnp.mean(jnp.square(x - mu), axis=-1, keepdims=True)
            return (x - mu) * jax.lax.rsqrt(var + EPS) * g + b
        key = jax.random.key(seed)
        ks = jax.random.split(key, 6)
        D, R, B, T = (128, 32, 8, 512)
        x = jax.random.normal(ks[0], (B, T, D), dtype=jnp.float32)
        qweights = jax.random.randint(ks[1], (6, D, D), 0, 16, dtype=jnp.int32)
        scales = jax.random.uniform(ks[2], (6, D, D // GROUP), dtype=jnp.float32)
        biases = jax.random.normal(ks[3], (6, D), dtype=jnp.float32) * 0.02
        lora_a = jax.random.normal(ks[4], (6, R, D), dtype=jnp.float32) * 0.02
        lora_b = jax.random.normal(ks[5], (6, D, R), dtype=jnp.float32) * 0.02
        ln_gamma = jnp.ones((3, D), dtype=jnp.float32)
        ln_beta = jnp.zeros((3, D), dtype=jnp.float32)
        return {'x': x, 'qweights': qweights, 'scales': scales, 'biases': biases, 'lora_a': lora_a, 'lora_b': lora_b, 'ln_gamma': ln_gamma, 'ln_beta': ln_beta}
    _L0_ffn_all = _L0_ffn_setup()
    _L0_ffn_in = {k: v for k, v in _L0_ffn_all.items() if k in ('qweights', 'scales', 'biases', 'lora_a', 'lora_b', 'ln_gamma', 'ln_beta')}
    del _L0_ffn_all

    def _L1_xattn_setup():
        import jax, jax.numpy as jnp
        import numpy as np
        DIM = 128
        NH = 8
        HD = DIM // NH
        E = 8
        EPS = 1e-05

        def rope_cos_sin(L, hd):
            inv_freq = 1.0 / 10000.0 ** (jnp.arange(0, hd, 2, dtype=jnp.float32) / hd)
            freqs = jnp.arange(L, dtype=jnp.float32)[:, None] * inv_freq[None, :]
            emb = jnp.concatenate([freqs, freqs], axis=-1)
            return (jnp.cos(emb), jnp.sin(emb))

        def rotate_half(x):
            x1 = x[..., 0::2]
            x2 = x[..., 1::2]
            return jnp.stack((-x2, x1), axis=-1).reshape(x.shape)

        def rope(t, cos, sin):
            return t * cos[None, None] + rotate_half(t) * sin[None, None]

        def heads(t):
            B, L, C = t.shape
            return t.reshape(B, L, NH, HD).transpose(0, 2, 1, 3)
        key = jax.random.key(seed)
        ks = jax.random.split(key, 32)
        std = 0.02
        d = {}
        d['x'] = jax.random.normal(ks[0], (16, 64, DIM), jnp.float32)
        d['h_a'] = jax.random.normal(ks[1], (16, 32, DIM), jnp.float32)
        d['h_t'] = jax.random.normal(ks[2], (16, 32, DIM), jnp.float32)
        names = ['qa', 'ka', 'va', 'qt', 'kt', 'vt', 'o', 'ffn']
        for i, n in enumerate(names):
            d['W_' + n] = jax.random.normal(ks[3 + 2 * i], (E, DIM, DIM), jnp.float32) * std
            d['b_' + n] = jax.random.normal(ks[4 + 2 * i], (E, DIM), jnp.float32) * std
        d['gamma'] = jnp.ones((E, DIM), jnp.float32)
        d['beta'] = jnp.zeros((E, DIM), jnp.float32)
        d['gating_factor'] = jnp.zeros((E,), jnp.float32)
        d['expert_idx'] = 3
        return d
    _L1_xattn_all = _L1_xattn_setup()
    _L1_xattn_in = {k: v for k, v in _L1_xattn_all.items() if k in ('W_qa', 'b_qa', 'W_ka', 'b_ka', 'W_va', 'b_va', 'W_qt', 'b_qt', 'W_kt', 'b_kt', 'W_vt', 'b_vt', 'W_o', 'b_o', 'W_ffn', 'b_ffn', 'gamma', 'beta', 'gating_factor')}
    del _L1_xattn_all

    def _L1_ffn_setup():
        import jax, jax.numpy as jnp
        import numpy as np
        BLOCK = 16
        _GRID = jnp.array([0.0, 0.5, 1.0, 1.5, 2.0, 3.0, 4.0, 6.0], dtype=jnp.float32)
        _MID = jnp.array([0.25, 0.75, 1.25, 1.75, 2.5, 3.5, 5.0], dtype=jnp.float32)

        def fp4_quant_dequant(x):
            shape = x.shape
            xb = x.reshape(shape[:-1] + (shape[-1] // BLOCK, BLOCK))
            scale = jnp.max(jnp.abs(xb), axis=-1, keepdims=True) / 6.0
            scale = jnp.maximum(scale, jnp.float32(1e-12))
            xn = xb / scale
            idx = jnp.searchsorted(_MID, jnp.abs(xn))
            q = _GRID[idx] * jnp.sign(xn) * scale
            return q.reshape(shape)

        def fp4_linear(x, w):
            xq = fp4_quant_dequant(x)
            wq = fp4_quant_dequant(w)
            return jnp.einsum('bsk,nk->bsn', xq, wq)
        key = jax.random.key(seed)
        k1, k2, k3, k4 = jax.random.split(key, 4)
        H, I = (128, 352)
        x = jax.random.normal(k1, (4, 512, H), dtype=jnp.float32)
        w_gate = jax.random.normal(k2, (I, H), dtype=jnp.float32) * 0.02
        w_up = jax.random.normal(k3, (I, H), dtype=jnp.float32) * 0.02
        w_down = jax.random.normal(k4, (H, I), dtype=jnp.float32) * 0.02
        return {'x': x, 'w_gate': w_gate, 'w_up': w_up, 'w_down': w_down}
    _L1_ffn_all = _L1_ffn_setup()
    _L1_ffn_in = {k: v for k, v in _L1_ffn_all.items() if k in ('w_gate', 'w_up', 'w_down')}
    del _L1_ffn_all
    return {'x': x, 'ctx_1024': ctx_1024, 'mask_BxS2_bk0': mask_BxS2_bk0, 'L0_xattn_ln_x_w': _L0_xattn_in['ln_x_w'], 'L0_xattn_ln_x_b': _L0_xattn_in['ln_x_b'], 'L0_xattn_ln_l_w': _L0_xattn_in['ln_l_w'], 'L0_xattn_ln_l_b': _L0_xattn_in['ln_l_b'], 'L0_xattn_Wq': _L0_xattn_in['Wq'], 'L0_xattn_Wkv': _L0_xattn_in['Wkv'], 'L0_xattn_q_scale': _L0_xattn_in['q_scale'], 'L0_xattn_k_scale': _L0_xattn_in['k_scale'], 'L0_xattn_Wo': _L0_xattn_in['Wo'], 'L0_xattn_ln_o_w': _L0_xattn_in['ln_o_w'], 'L0_xattn_ln_o_b': _L0_xattn_in['ln_o_b'], 'L0_ffn_qweights': _L0_ffn_in['qweights'], 'L0_ffn_scales': _L0_ffn_in['scales'], 'L0_ffn_biases': _L0_ffn_in['biases'], 'L0_ffn_lora_a': _L0_ffn_in['lora_a'], 'L0_ffn_lora_b': _L0_ffn_in['lora_b'], 'L0_ffn_ln_gamma': _L0_ffn_in['ln_gamma'], 'L0_ffn_ln_beta': _L0_ffn_in['ln_beta'], 'L1_xattn_W_qa': _L1_xattn_in['W_qa'], 'L1_xattn_b_qa': _L1_xattn_in['b_qa'], 'L1_xattn_W_ka': _L1_xattn_in['W_ka'], 'L1_xattn_b_ka': _L1_xattn_in['b_ka'], 'L1_xattn_W_va': _L1_xattn_in['W_va'], 'L1_xattn_b_va': _L1_xattn_in['b_va'], 'L1_xattn_W_qt': _L1_xattn_in['W_qt'], 'L1_xattn_b_qt': _L1_xattn_in['b_qt'], 'L1_xattn_W_kt': _L1_xattn_in['W_kt'], 'L1_xattn_b_kt': _L1_xattn_in['b_kt'], 'L1_xattn_W_vt': _L1_xattn_in['W_vt'], 'L1_xattn_b_vt': _L1_xattn_in['b_vt'], 'L1_xattn_W_o': _L1_xattn_in['W_o'], 'L1_xattn_b_o': _L1_xattn_in['b_o'], 'L1_xattn_W_ffn': _L1_xattn_in['W_ffn'], 'L1_xattn_b_ffn': _L1_xattn_in['b_ffn'], 'L1_xattn_gamma': _L1_xattn_in['gamma'], 'L1_xattn_beta': _L1_xattn_in['beta'], 'L1_xattn_gating_factor': _L1_xattn_in['gating_factor'], 'L1_ffn_w_gate': _L1_ffn_in['w_gate'], 'L1_ffn_w_up': _L1_ffn_in['w_up'], 'L1_ffn_w_down': _L1_ffn_in['w_down']}

def reference(x, ctx_1024, mask_BxS2_bk0, L0_xattn_ln_x_w, L0_xattn_ln_x_b, L0_xattn_ln_l_w, L0_xattn_ln_l_b, L0_xattn_Wq, L0_xattn_Wkv, L0_xattn_q_scale, L0_xattn_k_scale, L0_xattn_Wo, L0_xattn_ln_o_w, L0_xattn_ln_o_b, L0_ffn_qweights, L0_ffn_scales, L0_ffn_biases, L0_ffn_lora_a, L0_ffn_lora_b, L0_ffn_ln_gamma, L0_ffn_ln_beta, L1_xattn_W_qa, L1_xattn_b_qa, L1_xattn_W_ka, L1_xattn_b_ka, L1_xattn_W_va, L1_xattn_b_va, L1_xattn_W_qt, L1_xattn_b_qt, L1_xattn_W_kt, L1_xattn_b_kt, L1_xattn_W_vt, L1_xattn_b_vt, L1_xattn_W_o, L1_xattn_b_o, L1_xattn_W_ffn, L1_xattn_b_ffn, L1_xattn_gamma, L1_xattn_beta, L1_xattn_gating_factor, L1_ffn_w_gate, L1_ffn_w_up, L1_ffn_w_down):
    import jax
    import jax.numpy as jnp

    def _L0_xattn_ref(x, latents, mask, ln_x_w, ln_x_b, ln_l_w, ln_l_b, Wq, Wkv, q_scale, k_scale, Wo, ln_o_w, ln_o_b):
        import jax, jax.numpy as jnp
        import numpy as np
        DIM, DIM_HEAD, HEADS, SCALE = (128, 64, 8, 8.0)
        INNER = DIM_HEAD * HEADS
        LN_EPS = 1e-05
        L2_EPS = 1e-12

        def layer_norm(x, w, b):
            mu = jnp.mean(x, axis=-1, keepdims=True)
            var = jnp.mean(jnp.square(x - mu), axis=-1, keepdims=True)
            return (x - mu) * jax.lax.rsqrt(var + LN_EPS) * w + b

        def l2norm(t):
            n = jnp.sqrt(jnp.sum(jnp.square(t), axis=-1, keepdims=True))
            return t / jnp.maximum(n, L2_EPS)
        b, n, _ = x.shape
        m = latents.shape[1]
        x = layer_norm(x, ln_x_w, ln_x_b)
        latents = layer_norm(latents, ln_l_w, ln_l_b)
        q = latents @ Wq
        kv_input = jnp.concatenate([x, latents], axis=1)
        kv = kv_input @ Wkv
        k, v = jnp.split(kv, 2, axis=-1)

        def to_heads(t):
            return t.reshape(t.shape[0], t.shape[1], HEADS, DIM_HEAD).transpose(0, 2, 1, 3)
        q, k, v = map(to_heads, (q, k, v))
        q = l2norm(q) * q_scale
        k = l2norm(k) * k_scale
        sim = jnp.einsum('bhid,bhjd->bhij', q, k) * SCALE
        full_mask = jnp.concatenate([mask, jnp.ones((b, m), dtype=bool)], axis=1)[:, None, None, :]
        max_neg = -jnp.finfo(sim.dtype).max
        sim = jnp.where(full_mask, sim, max_neg)
        attn = jax.nn.softmax(sim.astype(jnp.float32), axis=-1).astype(sim.dtype)
        out = jnp.einsum('bhij,bhjd->bhid', attn, v)
        out = out.transpose(0, 2, 1, 3).reshape(b, m, INNER)
        return layer_norm(out @ Wo, ln_o_w, ln_o_b)

    def _L0_ffn_ref(x, qweights, scales, biases, lora_a, lora_b, ln_gamma, ln_beta):
        import jax, jax.numpy as jnp
        import numpy as np
        GROUP = 16
        EPS = 1e-05

        def _dequant(q, scale):
            w = q.astype(jnp.float32) / 7.5 - 1.0
            return w * jnp.repeat(scale, GROUP, axis=1)

        def _qlora_linear(x, q, scale, bias, la, lb):
            w = _dequant(q, scale)
            base = jnp.einsum('btd,od->bto', x, w) + bias
            lora = jnp.einsum('btr,or->bto', jnp.einsum('btd,rd->btr', x, la), lb)
            return base + lora

        def _layernorm(x, g, b):
            mu = jnp.mean(x, axis=-1, keepdims=True)
            var = jnp.mean(jnp.square(x - mu), axis=-1, keepdims=True)
            return (x - mu) * jax.lax.rsqrt(var + EPS) * g + b
        h = x
        for blk in range(3):
            i0, i1 = (2 * blk, 2 * blk + 1)
            y = _qlora_linear(h, qweights[i0], scales[i0], biases[i0], lora_a[i0], lora_b[i0])
            y = _layernorm(y, ln_gamma[blk], ln_beta[blk])
            y = jax.nn.gelu(y, approximate=False)
            y = _qlora_linear(y, qweights[i1], scales[i1], biases[i1], lora_a[i1], lora_b[i1])
            h = y + h
        return h

    def _L1_xattn_ref(x, h_a, h_t, W_qa, b_qa, W_ka, b_ka, W_va, b_va, W_qt, b_qt, W_kt, b_kt, W_vt, b_vt, W_o, b_o, W_ffn, b_ffn, gamma, beta, gating_factor, expert_idx):
        import jax, jax.numpy as jnp
        import numpy as np
        DIM = 128
        NH = 8
        HD = DIM // NH
        E = 8
        EPS = 1e-05

        def rope_cos_sin(L, hd):
            inv_freq = 1.0 / 10000.0 ** (jnp.arange(0, hd, 2, dtype=jnp.float32) / hd)
            freqs = jnp.arange(L, dtype=jnp.float32)[:, None] * inv_freq[None, :]
            emb = jnp.concatenate([freqs, freqs], axis=-1)
            return (jnp.cos(emb), jnp.sin(emb))

        def rotate_half(x):
            x1 = x[..., 0::2]
            x2 = x[..., 1::2]
            return jnp.stack((-x2, x1), axis=-1).reshape(x.shape)

        def rope(t, cos, sin):
            return t * cos[None, None] + rotate_half(t) * sin[None, None]

        def heads(t):
            B, L, C = t.shape
            return t.reshape(B, L, NH, HD).transpose(0, 2, 1, 3)
        e = expert_idx

        def lin(t, W, b):
            return t @ W[e].T + b[e]
        B, T, C = x.shape
        Ka = h_a.shape[1]
        Kt = h_t.shape[1]
        q_a = heads(lin(x, W_qa, b_qa))
        q_t = heads(lin(x, W_qt, b_qt))
        k_a = heads(lin(h_a, W_ka, b_ka))
        v_a = heads(lin(h_a, W_va, b_va))
        k_t = heads(lin(h_t, W_kt, b_kt))
        v_t = heads(lin(h_t, W_vt, b_vt))
        cos_m, sin_m = rope_cos_sin(T, HD)
        q_a = rope(q_a, cos_m, sin_m)
        q_t = rope(q_t, cos_m, sin_m)
        cos_a, sin_a = rope_cos_sin(Ka, HD)
        k_a = rope(k_a, cos_a, sin_a)
        cos_t, sin_t = rope_cos_sin(Kt, HD)
        k_t = rope(k_t, cos_t, sin_t)
        ratio_g = jax.nn.sigmoid(gating_factor[e])
        s_a = jnp.einsum('bhtd,bhkd->bhtk', q_a, k_a)
        s_t = jnp.einsum('bhtd,bhkd->bhtk', q_t, k_t) * ratio_g
        scores = jnp.concatenate([s_a, s_t], axis=-1) / np.sqrt(HD)
        w = jax.nn.softmax(scores, axis=-1)
        v = jnp.concatenate([v_a, v_t], axis=2)
        out = jnp.einsum('bhtk,bhkd->bhtd', w, v)
        out = out.transpose(0, 2, 1, 3).reshape(B, T, C)
        out = lin(out, W_o, b_o)
        x = out + x
        mu = jnp.mean(x, axis=-1, keepdims=True)
        var = jnp.var(x, axis=-1, keepdims=True)
        xn = (x - mu) / jnp.sqrt(var + EPS) * gamma[e] + beta[e]
        x = jax.nn.relu(lin(xn, W_ffn, b_ffn))
        return x

    def _L1_ffn_ref(x, w_gate, w_up, w_down):
        import jax, jax.numpy as jnp
        import numpy as np
        BLOCK = 16
        _GRID = jnp.array([0.0, 0.5, 1.0, 1.5, 2.0, 3.0, 4.0, 6.0], dtype=jnp.float32)
        _MID = jnp.array([0.25, 0.75, 1.25, 1.75, 2.5, 3.5, 5.0], dtype=jnp.float32)

        def fp4_quant_dequant(x):
            shape = x.shape
            xb = x.reshape(shape[:-1] + (shape[-1] // BLOCK, BLOCK))
            scale = jnp.max(jnp.abs(xb), axis=-1, keepdims=True) / 6.0
            scale = jnp.maximum(scale, jnp.float32(1e-12))
            xn = xb / scale
            idx = jnp.searchsorted(_MID, jnp.abs(xn))
            q = _GRID[idx] * jnp.sign(xn) * scale
            return q.reshape(shape)

        def fp4_linear(x, w):
            xq = fp4_quant_dequant(x)
            wq = fp4_quant_dequant(w)
            return jnp.einsum('bsk,nk->bsn', xq, wq)
        gate = fp4_linear(x, w_gate)
        y = fp4_linear(x, w_up)
        h = jax.nn.silu(gate) * y
        return fp4_linear(h, w_down)
    x = x + _L0_xattn_ref(ctx_1024, _layernorm(x, axis=-1), mask_BxS2_bk0, L0_xattn_ln_x_w, L0_xattn_ln_x_b, L0_xattn_ln_l_w, L0_xattn_ln_l_b, L0_xattn_Wq, L0_xattn_Wkv, L0_xattn_q_scale, L0_xattn_k_scale, L0_xattn_Wo, L0_xattn_ln_o_w, L0_xattn_ln_o_b)
    x = x + _L0_ffn_ref(_layernorm(x, axis=-1), L0_ffn_qweights, L0_ffn_scales, L0_ffn_biases, L0_ffn_lora_a, L0_ffn_lora_b, L0_ffn_ln_gamma, L0_ffn_ln_beta)
    x = x + _L1_xattn_ref(_layernorm(x, axis=-1), ctx_1024, ctx_1024, L1_xattn_W_qa, L1_xattn_b_qa, L1_xattn_W_ka, L1_xattn_b_ka, L1_xattn_W_va, L1_xattn_b_va, L1_xattn_W_qt, L1_xattn_b_qt, L1_xattn_W_kt, L1_xattn_b_kt, L1_xattn_W_vt, L1_xattn_b_vt, L1_xattn_W_o, L1_xattn_b_o, L1_xattn_W_ffn, L1_xattn_b_ffn, L1_xattn_gamma, L1_xattn_beta, L1_xattn_gating_factor, 3)
    x = x + _L1_ffn_ref(_layernorm(x, axis=-1), L1_ffn_w_gate, L1_ffn_w_up, L1_ffn_w_down)
    return x

_drawn_inputs = setup_inputs


def setup_inputs(seed=0):
    import zlib

    import numpy as np

    out = dict(_drawn_inputs(seed))
    spreads = {'L0_xattn_ln_x_w': (1.0, 0.2),
     'L0_xattn_ln_x_b': (0.0, 0.1),
     'L0_xattn_ln_l_w': (1.0, 0.2),
     'L0_xattn_ln_l_b': (0.0, 0.1),
     'L0_xattn_q_scale': (1.0, 0.2),
     'L0_xattn_k_scale': (1.0, 0.2),
     'L0_xattn_ln_o_w': (1.0, 0.2),
     'L0_xattn_ln_o_b': (0.0, 0.1),
     'L0_ffn_ln_gamma': (1.0, 0.2),
     'L0_ffn_ln_beta': (0.0, 0.1),
     'L1_xattn_gamma': (1.0, 0.6),
     'L1_xattn_beta': (0.0, 0.8),
     'L1_xattn_gating_factor': (0.0, 0.8)}
    factors = {'L0_ffn_biases': 5.303,
     'L0_ffn_lora_a': 5.569,
     'L0_ffn_lora_b': 5.719,
     'L1_xattn_W_qa': 8.0,
     'L1_xattn_b_qa': 8.0,
     'L1_xattn_W_ka': 8.0,
     'L1_xattn_b_ka': 8.0,
     'L1_xattn_W_va': 8.0,
     'L1_xattn_b_va': 8.0,
     'L1_xattn_W_qt': 8.0,
     'L1_xattn_b_qt': 8.0,
     'L1_xattn_W_kt': 8.0,
     'L1_xattn_b_kt': 8.0,
     'L1_xattn_W_vt': 8.0,
     'L1_xattn_b_vt': 8.0,
     'L1_xattn_W_o': 8.0,
     'L1_xattn_b_o': 8.0,
     'L1_xattn_b_ffn': 8.0,
     'L1_ffn_w_gate': 8.0,
     'L1_ffn_w_up': 8.0,
     'L1_ffn_w_down': 8.0}
    for name, (base, spread) in spreads.items():
        noise = np.random.default_rng([zlib.crc32(name.encode()), seed]).standard_normal(out[name].shape)
        drawn = base * np.exp(spread * noise) if base else spread * noise
        out[name] = jnp.asarray(drawn.astype(out[name].dtype))
    for name, factor in factors.items():
        out[name] = (out[name] * factor).astype(out[name].dtype)
    return out
```

```python
import math
from contextlib import ExitStack

import numpy as np

import concourse.bass as bass
from concourse import mybir
from concourse.alu_op_type import AluOpType as ALU

F32, F32R, BF16 = mybir.dt.float32, mybir.dt.float32r, mybir.dt.bfloat16
ACT = mybir.ActivationFunctionType
AX = mybir.AxisListType

P = 128
B = 8
D = 128
H = 8
DH0 = 64
DH1 = D // H
PAIRS = H // 2
EXPERT = 3
EPS = 1e-5
SCALE0 = 8.0
GROUP = 16
RANK = 32
NLIN = 6
FF = 352
FB = FF // GROUP
MASKED = 3.0e38
SPLIT = float(2 ** 22 + 1)
HALVES = 1.5 * 2 ** 22
VN = 96
V0 = DH0 + 1
V1 = DH1 + 1
W0 = H * V0 + VN - V0
W1 = H * V1 + VN - V1

(R_BIAS, R_GAMMA, R_BETA, R_LNXW, R_LNXB, R_LNLW, R_LNLB, R_QS, R_KS, R_BQA, R_BQT, R_BKA, R_BKT,
 R_G1, R_B1, R_LNOW, R_LNOB, R_BVA, R_BVT, R_BO, R_BFFN) = (
    0, 6, 9, 12, 13, 14, 15, 16, 17, 18, 19, 20, 21, 22, 23, 24, 25, 26, 27, 28, 29)
NVEC = 30
C_ID, C_ROPE, C_HM, C_GH, C_ROW0, C_M4 = 0, 128, 640, 648, 904, 1032
NCONST = 1036
QA, QT, KA, KT, VA, VT, WO, WF = range(8)


def count(t, k=0, n=1):
    return n * (t + 2) + k + 1


def build(nc, x, ctx, mask, wq, wkv, wo, qweights, qscales, lora_a, lora_b, vecs, ropebias, w1, gating,
          w_gate, w_up, w_down, consts, out):
    es = ExitStack()
    with es:
        def sb(name, shape, dt=F32):
            return es.enter_context(nc.sbuf_tensor(name, shape, dt))

        def pb(name, cols):
            return es.enter_context(nc.psum_tensor(name, [P, cols], F32))

        def sem(name):
            return es.enter_context(nc.semaphore(name))

        credits = []

        def loop_sem(name, n=1):
            s = sem(name)
            credits.append((s, 2 * n))
            return s

        cst = sb("cst", [P, NCONST])
        ident = cst[:, C_ID:C_ID + P]
        rope = cst[:, C_ROPE:C_ROPE + 4 * P].rearrange("p (k n) -> p k n", k=4)
        headmask = cst[:, C_HM:C_HM + H]
        ident_bf = sb("ident_bf", [P, P], BF16)
        grouphot = sb("grouphot", [P, 2, P], BF16)
        row0hot = sb("row0hot", [P, P], BF16)
        x_rows = sb("x_rows", [P, B, D])
        c_rows = sb("c_rows", [P, B, D])
        wq_s = sb("wq_s", [P, H * DH0])
        wkv_s = sb("wkv_s", [P, 2 * H * DH0])
        wo_s = sb("wo_s", [P, PAIRS, D])
        vec_rows = sb("vec_rows", [NVEC, P])
        vcol = sb("vcol", [P, NVEC])
        rb_rows = sb("rb_rows", [4, P])
        rb_rot = sb("rb_rot", [4, P])
        rbcol = sb("rbcol", [P, 4])
        kscol = sb("kscol", [P, 1])
        bc = sb("bc", [P, 10, P])
        BC_B1, BC_LNOW, BC_LNOB, BC_BVA, BC_BO, BC_BFFN = 0, 3, 4, 5, 7, 8
        mask_u8 = sb("mask_u8", [B, P], mybir.dt.uint8)
        maskr_u8 = sb("maskr_u8", [1, B * P], mybir.dt.uint8)
        mask_f = sb("mask_f", [B, P])
        maskcol = sb("maskcol", [P, B])
        maskrow = sb("maskrow", [P, B, 2 * P], BF16)
        stat = sb("stat", [P, 16, 6])
        mv = sb("mv", [P, 16, 2])
        rstd = sb("rstd", [P, 16])
        vpe = sb("vpe", [P, 16])
        mhalf = sb("mhalf", [P, 3 * H])
        cn = sb("cn", [P, 2, D])
        xl = sb("xl", [P, 2, D])
        cT = [sb(f"cT{i}", [P, P]) for i in range(2)]
        lT = [sb(f"lT{i}", [P, P]) for i in range(2)]
        big1 = sb("big1", [P, B * 3 * H * DH0])
        raw = big1[:, :].rearrange("p (b k n) -> p b k n", b=B, k=3)
        big2 = sb("big2", [P, B * 2 * W0])
        v0 = big2[:, :].rearrange("p (b c n) -> p b c n", b=B, c=2)
        v1 = big2[:, 0:B * 2 * W1].rearrange("p (b c n) -> p b c n", b=B, c=2)
        ssq = sb("ssq", [P, B, 3 * H])
        rn = sb("rn", [P, B, 3 * H])
        qkn = [sb(f"qkn{i}", [P, 3, H * DH0]) for i in range(2)]
        kT_hi = [sb(f"kT_hi{i}", [P, PAIRS, 2 * P], F32R) for i in range(2)]
        kT_lo = [sb(f"kT_lo{i}", [P, PAIRS, 2 * P], F32R) for i in range(2)]
        qz_hi = [sb(f"qz_hi{i}", [P, PAIRS, 2, P], F32R) for i in range(2)]
        qz_lo = [sb(f"qz_lo{i}", [P, PAIRS, 2, P], F32R) for i in range(2)]
        negmax = [sb(f"negmax{i}", [P, H], BF16) for i in range(2)]
        mblk = [sb(f"mblk{i}", [P, 4, P], BF16) for i in range(2)]
        pe_room = sb("pe_room", [P, 2 * H * P])
        probs = [pe_room[:, c * H * P:(c + 1) * H * P].rearrange("p (h n) -> p h n", h=H) for c in range(2)]
        sq = pe_room[:, 0:3 * H * DH0]
        w_deq = pe_room[:, 0:NLIN * D].rearrange("p (l d) -> p l d", l=NLIN)
        rden = sb("rden", [P, H])
        o_rows = sb("o_rows", [P, H * DH0])
        oT = sb("oT", [P, PAIRS, P])
        y_rows = sb("y_rows", [P, B, D])

        qw_i = qkn[0][:, :, :].rearrange("p a b -> p (a b)")[:, 0:NLIN * D].bitcast(mybir.dt.int32)\
            .rearrange("p (l d) -> p l d", l=NLIN)
        qw_s = sb("qw_s", [P, NLIN, D // GROUP])
        la_s = pe_room[0:RANK, NLIN * D:2 * NLIN * D].rearrange("p (l d) -> p l d", l=NLIN)
        lb_rows = sb("lb_rows", [P, NLIN, RANK])
        lbT = sb("lbT", [RANK, NLIN, D])
        wffn = sb("wffn", [P, NLIN, D])
        w1_s = qkn[1][:, :, :].rearrange("p a b -> p (a b)")[:, 0:8 * D].rearrange("p (m d) -> p m d", m=8)
        w1T = sb("w1T", [P, 8, D])
        w1rot = sb("w1rot", [P, 4, D])
        gate = sb("gate", [P, 1])
        NWG = 6 * D + FF
        w4 = big2[:, 6512:6512 + NWG]
        w4q = big2[:, 7632:7632 + NWG]
        wguT = sb("wguT", [P, 2, FF])
        wdT = sb("wdT", [P, 3, D])
        am = sb("am", [P, 2 * FB * 4])
        sc4 = sb("sc4", [P, 2 * FB * 4])
        rs4 = sb("rs4", [P, 2 * FB * 4])
        hT = big1[:, 0:1024]
        ysb = [big1[:, 1024 + 512 * g:1536 + 512 * g] for g in range(2)]
        yn = [big1[:, 2048 + 512 * g:2560 + 512 * g] for g in range(2)]
        gT = [big1[:, 3072 + 512 * g:3584 + 512 * g] for g in range(2)]
        x3T = big1[:, 4096:5120]
        ctxT = big1[:, 5120:6144]
        rope_t = [big1[:, 6144 + 512 * i:6656 + 512 * i] for i in range(4)]
        rows_n = big1[:, 6144:7168].rearrange("p (b d) -> p b d", b=B)
        q_hl = big1[:, 0:4096].rearrange("p (k n) -> p k n", k=4)
        k_hl = big1[:, 8192:12288].rearrange("p (b k n) -> p b k n", b=B, k=4)
        k_bf = wkv_s[:, :].bitcast(BF16).rearrange("p (k n) -> p k n", k=2)
        k_st = [sb(f"k_st{i}", [P, 4, P], F32R) for i in range(2)]
        q_bf = [big2[:, 3440 + 1024 * i:4464 + 1024 * i].bitcast(BF16).rearrange("p (k h n) -> p k h n", k=2, h=H)
                for i in range(2)]
        x3b = big2[:, 5488:6512].rearrange("p (b d) -> p b d", b=B)
        qblk = [[t[i][:, :, :, :].rearrange("p a e n -> p (a e n)") if t is qz_hi or t is qz_lo
                 else t[i][:, :, :].rearrange("p a n -> p (a n)") for t in (qz_hi, qz_lo, kT_hi, kT_lo)]
                for i in range(2)]
        z_rows = y_rows
        CW = (P, P, FF - 2 * P)
        xq = big1[:, 1024:2048]
        xqT = [big1[:, 2048 + 512 * g:2560 + 512 * g] for g in range(2)]
        sil = [big1[:, 3072 + FF * i:3072 + FF * (i + 1)] for i in range(2)]
        hidden = [big1[:, 4096 + 2 * FF * i:4096 + 2 * FF * (i + 1)] for i in range(2)]
        hq = [big2[:, 4208 + 2 * FF * i:4208 + 2 * FF * (i + 1)] for i in range(2)]
        hqT = [big2[:, 3440 + 384 * i:3824 + 384 * i] for i in range(2)]
        q_tmp = [big1[:, 7168 + NWG * i:7168 + NWG * (i + 1)] for i in range(4)]

        R = [pb(f"ring{i}", 512) for i in range(2)]
        S = [pb(f"scores{c}", 1024) for c in range(2)]
        O = [pb(f"outs{i}", 512) for i in range(2)]
        banks = [R[0][:, :], R[1][:, :], S[0][:, 0:512], S[0][:, 512:1024], S[1][:, 0:512],
                 S[1][:, 512:1024], O[0][:, :], O[1][:, :]]

        ld = {n: sem(f"ld_{n}") for n in ("cst", "ctx", "x", "vec", "bc", "mask", "wkv", "wq", "wo", "ffn",
                                          "lora", "w1", "fp4")}
        stored = sem("stored")
        vchain = sem("vchain")
        zeroed = sem("zeroed")
        prep_ps = sem("prep_ps")
        prep_v = sem("prep_v")
        powed = sem("powed")
        statd = sem("statd")
        ln_ready = loop_sem("ln_ready")
        xposed = loop_sem("xposed")
        lnT_ready = loop_sem("lnT_ready", 2)
        projected = loop_sem("projected", 5)
        squared = loop_sem("squared", 3)
        copied = loop_sem("copied", 3)
        v_saved = loop_sem("v_saved", 2)
        summed = loop_sem("summed")
        normed = loop_sem("normed")

        class Att:
            def __init__(self, n):
                self.input_ready = loop_sem(f"{n}_input_ready")
                self.input_ready2 = loop_sem(f"{n}_input_ready2")
                self.xposed = loop_sem(f"{n}_xposed", 3)
                self.hi_ready = loop_sem(f"{n}_hi_ready", 3)
                self.lo_ready = loop_sem(f"{n}_lo_ready", 3)
                self.scored = loop_sem(f"{n}_scored", 4)
                self.maxed = loop_sem(f"{n}_maxed", 4)
                self.maxT = loop_sem(f"{n}_maxT")
                self.mblk_ready = loop_sem(f"{n}_mblk_ready")
                self.shifted = loop_sem(f"{n}_shifted", 2)
                self.expd = loop_sem(f"{n}_expd", 2)
                self.mixed = loop_sem(f"{n}_mixed", 2)
                self.rdend = loop_sem(f"{n}_rdend", 2)
                self.divided = loop_sem(f"{n}_divided", 2)
                self.oT_ps = loop_sem(f"{n}_oT_ps")
                self.oT_ready = loop_sem(f"{n}_oT_ready")
                self.y_ps = loop_sem(f"{n}_y_ps")
                self.y_ready = loop_sem(f"{n}_y_ready")

        A = Att("a0")
        C = Att("a1")
        OT_BANK = {A: 0, C: 1}
        prep_a = sem("prep_a")
        rows_ready = sem("rows_ready")
        rowsT_ps = sem("rowsT_ps")
        rowsT = sem("rowsT")
        up_ps = sem("up_ps")
        up_norm = sem("up_norm")
        upT_ps = sem("upT_ps")
        gelu = sem("gelu")
        down_ps = sem("down_ps")
        h_ready = sem("h_ready")
        hrows_ps = sem("hrows_ps")
        x2_ready = sem("x2_ready")
        ctxT_ps = sem("ctxT_ps")
        ctxT_rdy = sem("ctxT_rdy")
        v1_ps = sem("v1_ps")
        v1_rdy = sem("v1_rdy")
        rope_ps = sem("rope_ps")
        rope_sum = sem("rope_sum")
        rope_hi = sem("rope_hi")
        rope_rdy = sem("rope_rdy")
        kbf_rdy = sem("kbf_rdy")
        v1_ones = sem("v1_ones")
        w4_zero = sem("w4_zero")
        w4q_rdy = sem("w4q_rdy")
        w4T_ps = sem("w4T_ps")
        w4T_rdy = sem("w4T_rdy")
        ff_ps = sem("ff_ps")
        x4_rdy = sem("x4_rdy")
        xq_rdy = sem("xq_rdy")
        xqT_ps = sem("xqT_ps")
        xqT_rdy = sem("xqT_rdy")
        gu_ps = sem("gu_ps")
        silu = sem("silu")
        hid = sem("hid")
        hq_rdy = sem("hq_rdy")
        hqT_ps = sem("hqT_ps")
        hqT_rdy = sem("hqT_rdy")
        dn_ps = sem("dn_ps")
        out_rdy = sem("out_rdy")

        block = es.enter_context(nc.Block())

        @block.sync
        def _(sp):
            for s, n in credits:
                sp.sem_inc(s, n)
            c_src, x_src = ctx.rearrange("b t d -> t b d"), x.rearrange("b t d -> t b d")
            sp.dma_start(c_rows[:, :, :], c_src).then_inc(ld["ctx"], 16)
            sp.dma_start(x_rows[:, :, :], x_src).then_inc(ld["x"], 16)
            sp.dma_start(wkv_s[:, :], wkv).then_inc(ld["wkv"], 16)
            sp.dma_start(wq_s[:, :], wq).then_inc(ld["wq"], 16)
            sp.dma_start(wo_s[:, :, :], wo.rearrange("(c p) n -> p c n", p=P)).then_inc(ld["wo"], 16)
            sp.dma_start(qw_i, qweights.rearrange("l o i -> o l i")).then_inc(ld["ffn"], 16)
            sp.dma_start(qw_s[:, :, :], qscales.rearrange("l o g -> o l g")).then_inc(ld["ffn"], 16)
            sp.dma_start(la_s, lora_a.rearrange("l r i -> r l i")).then_inc(ld["lora"], 16)
            sp.dma_start(lb_rows[:, :, :], lora_b.rearrange("l o r -> o l r")).then_inc(ld["lora"], 16)
            sp.dma_start(w1_s, w1.rearrange("m o i -> o m i")).then_inc(ld["w1"], 16)
            sp.dma_start(gate[:, :], gating.partition_broadcast(P)).then_inc(ld["w1"], 16)
            sp.wait_ge(w4_zero, 1)
            for k, w in enumerate((w_gate, w_up)):
                sp.dma_start(w4[:, 384 * k:384 * k + 256].rearrange("p (c i) -> p c i", c=2),
                             w[0:256, :].rearrange("(c p) i -> p c i", p=P)).then_inc(ld["fp4"], 16)
                sp.dma_start(w4[0:FF - 256, 384 * k + 256:384 * k + 384], w[256:FF, :]).then_inc(ld["fp4"], 16)
            sp.dma_start(w4[:, 768:NWG], w_down).then_inc(ld["fp4"], 16)
            for t in range(B):
                sp.wait_ge(out_rdy, t + 1)
                sp.dma_start(out[t, :, :], x_rows[:, t, :]).then_inc(stored, 16)
            sp.wait_ge(stored, 16 * B)

        @block.gpsimd
        def _(pool):
            nc.gpsimd.memset(mhalf[:, :], -0.5)
            for i in range(2):
                nc.gpsimd.memset(mblk[i][:, :, :], 0.0)
            nc.gpsimd.memset(maskrow[:, :, :], 0.0).then_inc(zeroed, 1)
            for i in range(2):
                nc.gpsimd.memset(qz_hi[i][:, :, :, :].bitcast(F32), 0.0)
                nc.gpsimd.memset(qz_lo[i][:, :, :, :].bitcast(F32), 0.0)
            nc.gpsimd.memset(v0, 0.0).then_inc(zeroed, 1)
            pool.wait_ge(zeroed, 2)
            nc.gpsimd.memset(v0[:, :, :, 0:H * V0].rearrange("p b c (h n) -> p (b c) h n", n=V0)[:, :, :, DH0:V0],
                             1.0).then_inc(zeroed, 1)
            pool.wait_ge(zeroed, 3)
            pool.wait_ge(statd, 1)
            nc.gpsimd.tensor_tensor(rstd[:, :], vpe[:, :], mhalf[:, 0:16], ALU.pow).then_inc(powed, 1)

            def norms(t):
                pool.wait_ge(summed, count(t))
                nc.gpsimd.tensor_tensor(rn[:, t, :], ssq[:, t, :], mhalf[:, :], ALU.pow).then_inc(normed, 1)

            with pool.Fori(0, B) as t:
                norms(t)

            def scale_qk(t, par):
                pool.wait_ge(A.xposed, count(t - 2, 2, 3))
                nc.gpsimd.tensor_tensor(
                    qkn[par][:, :, :].rearrange("p k (h d) -> p (k h) d", d=DH0),
                    raw[:, t, :, :].rearrange("p k (h d) -> p (k h) d", d=DH0),
                    rn[:, t, :].unsqueeze(2).broadcast_to([P, 3 * H, DH0]), ALU.mult).then_inc(A.input_ready, 1)

            pool.wait_ge(normed, count(B - 1))
            with pool.Fori(0, B // 2) as i:
                scale_qk(2 * i, 0)
                scale_qk(2 * i + 1, 1)

            pool.wait_ge(A.y_ready, count(B - 1))
            nc.gpsimd.memset(w4, 0.0).then_inc(w4_zero, 1)
            nc.gpsimd.memset(v1, 0.0).then_inc(v1_ones, 1)
            pool.wait_ge(v1_ones, 1)
            nc.gpsimd.memset(v1[:, :, :, 0:H * V1].rearrange("p b c (h n) -> p (b c) h n", n=V1)[:, :, :, DH1:V1],
                             1.0).then_inc(v1_ones, 1)

            def inverse_deviation(n, at, width):
                pool.wait_ge(statd, n)
                nc.gpsimd.tensor_tensor(rstd[:, at:at + width], vpe[:, at:at + width], mhalf[:, 0:width], ALU.pow)\
                    .then_inc(powed, 1)

            inverse_deviation(2, 0, B)
            inverse_deviation(3, 0, B)
            for n in range(6):
                inverse_deviation(4 + n, 4 * (n % 2), 4)
            inverse_deviation(10, 0, B)

            def stage_operands(t, par):
                pool.wait_ge(C.shifted, count(t - 2, 1, 2))
                nc.gpsimd.tensor_copy(k_st[par][:, :, :], k_hl[:, t, :, :]).then_inc(C.input_ready2, 1)
                for kind in (1, 3):
                    last = nc.gpsimd.tensor_tensor(
                        qblk[par][kind].rearrange("p (h n) -> p h n", h=H),
                        q_hl[:, kind, bass.ds(t * P, P)].unsqueeze(1).broadcast_to([P, H, P]),
                        headmask.unsqueeze(2).broadcast_to([P, H, P]), ALU.mult)
                last.then_inc(C.lo_ready, 3)

            pool.wait_ge(rope_rdy, 8)
            with pool.Fori(0, B // 2) as i:
                stage_operands(2 * i, 0)
                stage_operands(2 * i + 1, 1)
            inverse_deviation(11, 0, B)
            inverse_deviation(12, 0, B)

        @block.scalar
        def _(act):
            act.dma_start(cst[:, :], consts).then_inc(ld["cst"], 16)
            act.dma_start(vec_rows[:, :], vecs).then_inc(ld["vec"], 16)
            act.dma_start(rb_rows[:, :], ropebias).then_inc(ld["vec"], 16)
            act.dma_start(mask_u8[:, :], mask).then_inc(ld["mask"], 16)
            act.dma_start(maskr_u8[:, :], mask.rearrange("(o b) t -> o (b t)", o=1)).then_inc(ld["mask"], 16)
            for k, (row, n) in enumerate(((R_BIAS, 1), (R_BIAS + 2, 1), (R_BIAS + 4, 1), (R_LNOW, 6))):
                act.dma_start(bc[:, k:k + n, :], vecs[row:row + n, :].partition_broadcast(P)).then_inc(ld["bc"], 16)

            def operands(t, par):
                act.wait_ge(xposed, count(t))
                act.wait_ge(projected, count(t - 2, 1, 5))
                nc.scalar.activation(cT[par][:, :], R[par][:, 0:P], ACT.Identity, bias=vcol[:, R_LNXB:R_LNXB + 1],
                                     scale=vcol[:, R_LNXW:R_LNXW + 1]).then_inc(lnT_ready, 1)
                act.wait_ge(projected, count(t - 2, 4, 5))
                nc.scalar.activation(lT[par][:, :], R[par][:, P:2 * P], ACT.Identity, bias=vcol[:, R_LNLB:R_LNLB + 1],
                                     scale=vcol[:, R_LNLW:R_LNLW + 1]).then_inc(lnT_ready, 1)

            def save_v(t, half):
                act.wait_ge(projected, count(t, (1, 4)[half], 5))
                nc.scalar.activation(
                    v0[:, t, half, 0:H * V0].rearrange("p (h n) -> p h n", n=V0)[:, :, 0:DH0],
                    banks[(3, 6)[half]].rearrange("p (h d) -> p h d", d=DH0), ACT.Copy).then_inc(v_saved, 1)

            def square(t, k):
                act.wait_ge(projected, count(t, (0, 2, 3)[k], 5))
                act.wait_ge(summed, count(t - 1))
                nc.scalar.activation(sq[:, k * 512:(k + 1) * 512], banks[(2, 4, 5)[k]], ACT.Square)\
                    .then_inc(squared, 1)

            def project_acts(t, par, more):
                square(t, 0)
                save_v(t, 0)
                if more:
                    operands(t + 1, 1 - par)
                square(t, 1)
                square(t, 2)
                save_v(t, 1)

            act.wait_ge(prep_ps, 2)
            nc.scalar.activation(lbT[:, 0:4, :], banks[6][0:RANK, :], ACT.Copy)
            nc.scalar.activation(lbT[:, 4:6, :], banks[7][0:RANK, 0:2 * D], ACT.Copy).then_inc(prep_a, 1)
            act.wait_ge(ld["w1"], 32)
            nc.scalar.activation(gate[:, :], gate[:, :], ACT.Exp, scale=-1.0).then_inc(prep_a, 1)
            act.wait_ge(prep_ps, 3)
            act.wait_ge(prep_v, 3)
            nc.scalar.activation(w1T[:, QA:KT, :], banks[2][:, 0:3 * D], ACT.Copy)
            nc.scalar.activation(w1T[:, KT, :], banks[2][:, 3 * D:4 * D], ACT.Copy, scale=gate[:, :])
            nc.scalar.activation(w1T[:, VA:WF + 1, :], banks[3], ACT.Copy).then_inc(prep_a, 1)
            act.wait_ge(prep_ps, 4)
            nc.scalar.activation(wffn[:, 0:4, :], banks[4], ACT.Copy)
            nc.scalar.activation(wffn[:, 4:6, :], banks[5][:, 0:2 * D], ACT.Copy).then_inc(prep_a, 1)

            act.wait_ge(prep_v, 1)
            act.wait_ge(zeroed, 3)
            operands(0, 0)
            with act.Fori(0, B // 2 - 1) as i:
                project_acts(2 * i, 0, True)
                project_acts(2 * i + 1, 1, True)
            project_acts(B - 2, 0, True)
            project_acts(B - 1, 1, False)

            def hi_k(t, par, half):
                act.wait_ge(A.xposed, count(t, half, 3))
                act.wait_ge(A.shifted, count(t - 2, 1, 2))
                nc.scalar.activation(kT_hi[par][:, :, half * P:(half + 1) * P],
                                     R[half][:, :].rearrange("p (k n) -> p k n", n=P), ACT.Copy,
                                     scale=kscol[:, :]).then_inc(A.hi_ready, 1)

            def hi_q(t, par):
                act.wait_ge(A.xposed, count(t, 2, 3))
                for e in range(2):
                    rows = slice(64 * e, 64 * e + 64)
                    last = nc.scalar.activation(qz_hi[par][rows, :, e, :],
                                                R[0][rows, :].rearrange("p (k n) -> p k n", n=P), ACT.Copy)
                last.then_inc(A.hi_ready, 1)

            def exponentials(a, t, half, bias):
                act.wait_ge(a.shifted, count(t, half, 2))
                act.wait_ge(a.mixed, count(t - 1, 1, 2))
                nc.scalar.activation(probs[half][:, :, :], S[half][:, :], ACT.Exp, bias=bias).then_inc(a.expd, 1)

            def outT(a, t, cols):
                act.wait_ge(a.oT_ps, count(t))
                act.wait_ge(a.y_ps, count(t - 1))
                nc.scalar.activation(oT[:, 0:cols // P, :], R[OT_BANK[a]][:, 0:cols], ACT.Copy).then_inc(a.oT_ready, 1)

            def attend0_front(t, par):
                hi_k(t, par, 0)

            def attend0(t, par, more):
                if more:
                    hi_k(t + 1, 1 - par, 0)
                exponentials(A, t, 0, maskcol[:, bass.ds(t, 1)])
                if more:
                    hi_k(t + 1, 1 - par, 1)
                    hi_q(t + 1, 1 - par)
                exponentials(A, t, 1, 0.0)
                outT(A, t, 512)
                act.wait_ge(A.y_ps, count(t))
                nc.scalar.activation(y_rows[:, t, :], R[1][:, 0:D], ACT.Copy).then_inc(A.y_ready, 1)

            hi_k(0, 0, 0)
            hi_k(0, 0, 1)
            hi_q(0, 0)
            with act.Fori(0, B // 2 - 1) as i:
                attend0(2 * i, 0, True)
                attend0(2 * i + 1, 1, True)
            attend0(B - 2, 0, True)
            attend0(B - 1, 1, False)

            def hidden_transposed(g):
                for t in (2 * g, 2 * g + 1):
                    act.wait_ge(hqT_ps, t + 1)
                    act.wait_ge(dn_ps, t - 1) if t >= 2 else None
                    nc.scalar.activation(hqT[t % 2][:, 0:2 * P], R[t % 2][:, 0:2 * P], ACT.Copy)
                    nc.scalar.activation(hqT[t % 2][0:CW[2], 2 * P:3 * P], R[t % 2][0:CW[2], 2 * P:3 * P],
                                         ACT.Copy).then_inc(hqT_rdy, 1)

            def rows_transposed(n, dst, scale=1.0, bias=0.0):
                act.wait_ge(rowsT_ps, n)
                for g in range(2):
                    last = nc.scalar.activation(dst[:, g * 512:(g + 1) * 512], R[g][:, :], ACT.Identity, bias=bias,
                                                scale=scale)
                last.then_inc(rowsT, 1)

            rows_transposed(1, hT)
            for blk in range(3):
                for g in range(2):
                    n = 2 * blk + g + 1
                    act.wait_ge(upT_ps, n)
                    nc.scalar.activation(gT[g], banks[4 + g], ACT.Gelu, bias=vcol[:, R_BETA + blk:R_BETA + blk + 1],
                                         scale=vcol[:, R_GAMMA + blk:R_GAMMA + blk + 1]).then_inc(gelu, 1)

            act.wait_ge(ctxT_ps, 1)
            for g in range(2):
                last = nc.scalar.activation(ctxT[:, g * 512:(g + 1) * 512], R[g][:, :], ACT.Copy)
            last.then_inc(ctxT_rdy, 1)
            rows_transposed(2, x3T)

            def upper(n):
                m, g = n // 2, n % 2
                act.wait_ge(rope_sum, n + 1)
                src = rope_t[2 * g]
                if m in (0, 1):
                    dst = k_hl[:, 4 * g:4 * g + 4, 2 * m, :]
                    nc.scalar.activation(dst.bitcast(F32R), src.rearrange("p (b n) -> p b n", n=P), ACT.Copy)
                    nc.scalar.activation(k_bf[:, m, g * 512:(g + 1) * 512], src, ACT.Copy).then_inc(rope_hi, 1)
                else:
                    nc.scalar.activation(q_hl[:, 2 * (m - 2), g * 512:(g + 1) * 512].bitcast(F32R), src, ACT.Copy)\
                        .then_inc(rope_hi, 1)

            for n in range(8):
                upper(n)

            def narrow_q(t, par):
                act.wait_ge(C.hi_ready, count(t, 2, 3))
                act.wait_ge(C.scored, count(t - 2, 3, 4))
                for k in range(2):
                    last = nc.scalar.activation(q_bf[par][:, k, :, :].rearrange("p h n -> p (h n)"),
                                                qblk[par][2 * k].bitcast(F32), ACT.Copy)
                last.then_inc(C.input_ready, 1)

            def attend1(t, par, more):
                exponentials(C, t, 0, 0.0)
                if more:
                    narrow_q(t + 1, 1 - par)
                exponentials(C, t, 1, 0.0)
                outT(C, t, P)

            narrow_q(0, 0)
            with act.Fori(0, B // 2 - 1) as i:
                attend1(2 * i, 0, True)
                attend1(2 * i + 1, 1, True)
            attend1(B - 2, 0, True)
            attend1(B - 1, 1, False)

            rows_transposed(3, hT, scale=vcol[:, R_G1:R_G1 + 1], bias=vcol[:, R_B1:R_B1 + 1])

            act.wait_ge(w4T_ps, 1)
            for k in range(2):
                for c, width in enumerate(CW):
                    nc.scalar.activation(wguT[:, k, c * P:c * P + width], banks[2 + k][:, c * P:c * P + width], ACT.Copy)
            for c, width in enumerate(CW):
                last = nc.scalar.activation(wdT[0:width, c, :], banks[4][0:width, c * P:(c + 1) * P], ACT.Copy)
            last.then_inc(w4T_rdy, 1)
            for g in range(2):
                act.wait_ge(xqT_ps, g + 1)
                nc.scalar.activation(xqT[g], R[g][:, :], ACT.Copy).then_inc(xqT_rdy, 1)
            for g in range(4):
                for t in (2 * g, 2 * g + 1):
                    act.wait_ge(gu_ps, t + 1)
                    nc.scalar.activation(sil[t % 2], banks[2 + 2 * (t % 2)][:, 0:FF], ACT.Silu).then_inc(silu, 1)
                if g >= 1:
                    hidden_transposed(g - 1)
            hidden_transposed(3)


        @block.vector
        def _(dve):
            done = [0]

            def link(ins, wait=True):
                ins.then_inc(vchain, 1)
                done[0] += 1
                if wait:
                    dve.wait_ge(vchain, done[0])

            dve.wait_ge(ld["cst"], 16)
            nc.vector.tensor_copy(ident_bf[:, :], ident)
            nc.vector.tensor_copy(grouphot[:, :, :], cst[:, C_GH:C_GH + 2 * P])
            nc.vector.tensor_copy(row0hot[:, :], cst[:, C_ROW0:C_ROW0 + P])
            dve.wait_ge(ld["mask"], 32)
            nc.vector.tensor_scalar(mask_f[:, :], mask_u8[:, :], MASKED, -MASKED, ALU.mult, ALU.add)
            dve.wait_ge(zeroed, 1)
            nc.vector.tensor_scalar(maskrow[0:1, :, 0:P], maskr_u8[:, :].rearrange("o (b t) -> o b t", b=B),
                                    MASKED, -MASKED, ALU.mult, ALU.add)
            dve.wait_ge(ld["vec"], 32)
            pairs = rb_rows[:, :].rearrange("p (i two) -> p i two", two=2)
            rot = rb_rot[:, :].rearrange("p (i two) -> p i two", two=2)
            nc.vector.tensor_scalar(rot[:, :, 0], pairs[:, :, 1], -1.0, None, ALU.mult)
            link(nc.vector.tensor_copy(rot[:, :, 1], pairs[:, :, 0]), wait=False)
            dve.wait_ge(prep_ps, 1)
            nc.vector.tensor_copy(vcol[:, :], R[0][:, 0:NVEC])
            nc.vector.tensor_copy(rbcol[:, :], R[0][:, 32:36])
            link(nc.vector.tensor_copy(maskcol[:, :], R[0][:, 40:40 + B]))
            nc.vector.scalar_tensor_tensor(out=kscol[:, :], in0=vcol[:, R_KS:R_KS + 1], scalar=SCALE0,
                                           in1=vcol[:, R_QS:R_QS + 1], op0=ALU.mult, op1=ALU.mult)\
                .then_inc(prep_v, 1)
            dve.wait_ge(ld["ctx"], 16)
            for t in range(B):
                nc.vector.bn_stats(stat[:, t, :], c_rows[:, t, :])
            dve.wait_ge(ld["x"], 16)
            for t in range(B):
                last = nc.vector.bn_stats(stat[:, B + t, :], x_rows[:, t, :])
            link(last)
            for t in range(2 * B):
                last = nc.vector.bn_aggr(mv[:, t, :], stat[:, t, :])
            link(last)
            nc.vector.tensor_scalar(vpe[:, 0:B], mv[:, 0:B, 1], EPS, None, ALU.add)
            nc.vector.tensor_scalar(vpe[:, B:2 * B], mv[:, B:2 * B, 1], 1.0 + EPS, EPS * EPS, ALU.mult, ALU.add)\
                .then_inc(statd, 1)
            dve.wait_ge(ld["ffn"], 32)
            link(nc.vector.tensor_scalar(w_deq, qw_i, 1.0 / 7.5, -1.0, ALU.mult, ALU.add))
            nc.vector.tensor_tensor(w_deq.rearrange("p l (g c) -> p (l g) c", c=GROUP),
                                    w_deq.rearrange("p l (g c) -> p (l g) c", c=GROUP),
                                    qw_s[:, :, :].rearrange("p l g -> p (l g)").unsqueeze(2)
                                    .broadcast_to([P, NLIN * D // GROUP, GROUP]), ALU.mult).then_inc(prep_v, 1)
            dve.wait_ge(prep_a, 2)
            link(nc.vector.tensor_scalar(gate[:, :], gate[:, :], 1.0, None, ALU.add))
            nc.vector.reciprocal(gate[:, :], gate[:, :]).then_inc(prep_v, 1)
            dve.wait_ge(prep_v, 3)
            nc.vector.tensor_tensor(vcol[:, R_BKT:R_BKT + 1], vcol[:, R_BKT:R_BKT + 1], gate[:, :], ALU.mult)
            nc.vector.tensor_tensor(rbcol[:, 3:4], rbcol[:, 3:4], gate[:, :], ALU.mult)
            dve.wait_ge(prep_a, 3)
            even_odd = w1T[:, QA:KT + 1, :].rearrange("p m (i two) -> p m i two", two=2)
            rotated = w1rot[:, :, :].rearrange("p m (i two) -> p m i two", two=2)
            nc.vector.tensor_scalar(rotated[:, :, :, 0], even_odd[:, :, :, 1], -1.0, None, ALU.mult)
            nc.vector.tensor_copy(rotated[:, :, :, 1], even_odd[:, :, :, 0]).then_inc(prep_v, 1)
            dve.wait_ge(powed, 1)

            def normalize(t, par):
                dve.wait_ge(xposed, count(t - 2))
                nc.vector.tensor_scalar(cn[:, par, :], c_rows[:, t, :], mv[:, t, 0:1], rstd[:, bass.ds(t, 1)],
                                        ALU.subtract, ALU.mult)
                nc.vector.tensor_scalar(xl[:, par, :], x_rows[:, t, :], mv[:, t + B, 0:1], rstd[:, bass.ds(t + B, 1)],
                                        ALU.subtract, ALU.mult).then_inc(ln_ready, 1)

            def save_qk(t, k):
                dve.wait_ge(squared, count(t, k, 3))
                nc.vector.tensor_copy(raw[:, t, k, :], banks[(2, 4, 5)[k]]).then_inc(copied, 1)

            def project_vecs(t, par, more):
                if more:
                    normalize(t + 1, 1 - par)
                for k in range(3):
                    save_qk(t, k)
                nc.vector.tensor_reduce(ssq[:, t, :], sq[:, :].rearrange("p (h d) -> p h d", d=DH0), axis=AX.X,
                                        op=ALU.add).then_inc(summed, 1)

            normalize(0, 0)
            with dve.Fori(0, B // 2 - 1) as i:
                project_vecs(2 * i, 0, True)
                project_vecs(2 * i + 1, 1, True)
            project_vecs(B - 2, 0, True)
            project_vecs(B - 1, 1, False)

            def lo_k(t, par, half):
                dve.wait_ge(A.hi_ready, count(t, half, 3))
                span = slice(half * P, (half + 1) * P)
                nc.vector.scalar_tensor_tensor(
                    out=kT_lo[par][:, :, span], in0=R[half][:, :].rearrange("p (k n) -> p k n", n=P),
                    scalar=kscol[:, :], in1=kT_hi[par][:, :, span].bitcast(F32), op0=ALU.mult,
                    op1=ALU.subtract).then_inc(A.lo_ready, 1)

            def lo_q(t, par):
                dve.wait_ge(A.hi_ready, count(t, 2, 3))
                for e in range(2):
                    rows = slice(64 * e, 64 * e + 64)
                    last = nc.vector.tensor_tensor(qz_lo[par][rows, :, e, :],
                                                   R[0][rows, :].rearrange("p (k n) -> p k n", n=P),
                                                   qz_hi[par][rows, :, e, :].bitcast(F32), ALU.subtract)
                last.then_inc(A.lo_ready, 1)

            def maximum(a, t, par, pair, bank):
                dve.wait_ge(a.scored, count(t, pair, 4))
                dve.wait_ge(a.maxT, count(t - 2))
                nc.vector.tensor_reduce(negmax[par][:, 2 * pair:2 * pair + 2],
                                        R[bank][:, :].rearrange("p (h n) -> p h n", h=2), axis=AX.X, op=ALU.max,
                                        negate=True).then_inc(a.maxed, 1)

            def max_operand(a, t, par, bank):
                dve.wait_ge(a.maxT, count(t))
                dve.wait_ge(a.shifted, count(t - 2, 1, 2))
                nc.vector.tensor_tensor(mblk[par][0:H, :, :],
                                        R[bank][0:H, 0:P].unsqueeze(1).broadcast_to([H, 4, P]),
                                        cst[0:H, C_M4:C_M4 + 4].unsqueeze(2).broadcast_to([H, 4, P]),
                                        ALU.mult).then_inc(a.mblk_ready, 1)

            def divide(a, t, g, dh):
                heads = O[g][:, 0:4 * VN].rearrange("p (h n) -> p h n", n=VN)
                dve.wait_ge(a.mixed, count(t, g, 2))
                nc.vector.reciprocal(rden[:, 4 * g:4 * g + 4], heads[:, :, dh]).then_inc(a.rdend, 1)
                dve.wait_ge(a.rdend, count(t, g, 2))
                dve.wait_ge(a.oT_ps, count(t - 1))
                nc.vector.tensor_tensor(
                    o_rows[:, 4 * g * dh:4 * (g + 1) * dh].rearrange("p (h d) -> p h d", d=dh), heads[:, :, 0:dh],
                    rden[:, 4 * g:4 * g + 4].unsqueeze(2).broadcast_to([P, 4, dh]), ALU.mult).then_inc(a.divided, 1)

            def attend0_vecs(t, par, more):
                if more:
                    lo_k(t + 1, 1 - par, 0)
                    lo_k(t + 1, 1 - par, 1)
                    lo_q(t + 1, 1 - par)
                    maximum(A, t + 1, 1 - par, 0, 1)
                    maximum(A, t + 1, 1 - par, 1, 0)
                divide(A, t, 0, DH0)
                if more:
                    maximum(A, t + 1, 1 - par, 2, 1)
                    maximum(A, t + 1, 1 - par, 3, 0)
                divide(A, t, 1, DH0)
                if more:
                    max_operand(A, t + 1, 1 - par, 1)

            lo_k(0, 0, 0)
            lo_k(0, 0, 1)
            lo_q(0, 0)
            for pair in range(4):
                maximum(A, 0, 0, pair, 1 - pair % 2)
            max_operand(A, 0, 0, 1)
            with dve.Fori(0, B // 2 - 1) as i:
                attend0_vecs(2 * i, 0, True)
                attend0_vecs(2 * i + 1, 1, True)
            attend0_vecs(B - 2, 0, True)
            attend0_vecs(B - 1, 1, False)

            def moments(src, at, tiles, eps_scale=1.0):
                for t in range(tiles):
                    last = nc.vector.bn_stats(stat[:, at + t, :], src[:, t, :])
                link(last)
                for t in range(tiles):
                    last = nc.vector.bn_aggr(mv[:, at + t, :], stat[:, at + t, :])
                link(last)
                nc.vector.tensor_scalar(vpe[:, at:at + tiles], mv[:, at:at + tiles, 1], EPS, None, ALU.add)\
                    .then_inc(statd, 1)

            def normalized(n, dst, src, at, tiles):
                dve.wait_ge(powed, n)
                for t in range(tiles):
                    last = nc.vector.tensor_scalar(dst[:, t, :], src[:, t, :], mv[:, at + t, 0:1],
                                                   rstd[:, at + t:at + t + 1], ALU.subtract, ALU.mult)
                return last

            def along(v, tiles=B):
                return v.unsqueeze(1).broadcast_to([P, tiles, P])

            def quantize(dst, src, n):
                blocks, u32 = n // GROUP, mybir.dt.uint32
                ratio, a, big, low = (t[:, 0:n] for t in q_tmp)
                as_blocks = lambda v: v.rearrange("p (b c) -> p b c", c=GROUP)
                spread = lambda v: v[:, 0:blocks].unsqueeze(2).broadcast_to([P, blocks, GROUP])
                link(nc.vector.tensor_reduce(am[:, 0:blocks], as_blocks(src), axis=AX.X, op=ALU.max,
                                             apply_absolute_value=True))
                link(nc.vector.tensor_scalar(sc4[:, 0:blocks], am[:, 0:blocks], 1.0 / 6.0, 1e-12, ALU.mult, ALU.max))
                link(nc.vector.reciprocal(rs4[:, 0:blocks], sc4[:, 0:blocks]))
                link(nc.vector.tensor_scalar(rs4[:, 0:blocks], rs4[:, 0:blocks], 1.0 - 2.0 ** -22, None, ALU.mult))
                link(nc.vector.tensor_tensor(as_blocks(ratio), as_blocks(src), spread(rs4), ALU.mult))
                link(nc.vector.tensor_scalar(a.bitcast(u32), ratio.bitcast(u32), 0x7FFFFFFF, None, ALU.bitwise_and))
                link(nc.vector.tensor_scalar(big, a, 1.0, None, ALU.max))
                link(nc.vector.scalar_tensor_tensor(out=low, in0=big, scalar=SPLIT, in1=big, op0=ALU.mult,
                                                    op1=ALU.subtract))
                link(nc.vector.scalar_tensor_tensor(out=big, in0=big, scalar=SPLIT, in1=low, op0=ALU.mult,
                                                    op1=ALU.subtract))
                link(nc.vector.tensor_scalar(a, a, 1.0, HALVES, ALU.min, ALU.add))
                link(nc.vector.scalar_tensor_tensor(out=a, in0=a, scalar=HALVES + 1.0, in1=big, op0=ALU.subtract,
                                                    op1=ALU.add))
                link(nc.vector.scalar_tensor_tensor(out=a.bitcast(u32), in0=ratio.bitcast(u32), scalar=0x80000000,
                                                    in1=a.bitcast(u32), op0=ALU.bitwise_and, op1=ALU.bitwise_or))
                return nc.vector.tensor_tensor(as_blocks(dst), as_blocks(a), spread(sc4), ALU.mult)

            dve.wait_ge(A.y_ready, count(B - 1))
            dve.wait_ge(ld["bc"], 64)
            moments(y_rows, 0, B)
            dve.wait_ge(ld["fp4"], 16 * 5)
            quantize(w4q, w4, NWG).then_inc(w4q_rdy, 1)
            link(normalized(2, rows_n, y_rows, 0, B))
            link(nc.vector.tensor_tensor(rows_n, rows_n, along(bc[:, BC_LNOW, :]), ALU.mult))
            link(nc.vector.tensor_tensor(rows_n, rows_n, along(bc[:, BC_LNOB, :]), ALU.add))
            link(nc.vector.tensor_tensor(x_rows[:, :, :], x_rows[:, :, :], rows_n, ALU.add))

            moments(x_rows, 0, B)
            normalized(3, rows_n, x_rows, 0, B).then_inc(rows_ready, 1)
            dve.wait_ge(rowsT, 1)
            for blk in range(3):
                for g in range(2):
                    n = 2 * blk + g + 1
                    rows = ysb[g].rearrange("p (t d) -> p t d", d=D)
                    dve.wait_ge(up_ps, n)
                    link(nc.vector.tensor_tensor(rows, banks[2 + g].rearrange("p (t d) -> p t d", d=D),
                                                 along(bc[:, BC_B1 + blk, :], 4), ALU.add))
                    moments(rows, 4 * g, 4)
                for g in range(2):
                    n = 2 * blk + g + 1
                    rows = ysb[g].rearrange("p (t d) -> p t d", d=D)
                    if n > 2:
                        dve.wait_ge(upT_ps, n - 2)
                    normalized(3 + n, yn[g].rearrange("p (t d) -> p t d", d=D), rows, 4 * g, 4).then_inc(up_norm, 1)
                for g in range(2):
                    n = 2 * blk + g + 1
                    dve.wait_ge(down_ps, n)
                    half = hT[:, g * 512:(g + 1) * 512]
                    nc.vector.scalar_tensor_tensor(out=half, in0=banks[6 + g],
                                                   scalar=vcol[:, R_BIAS + 2 * blk + 1:R_BIAS + 2 * blk + 2],
                                                   in1=half, op0=ALU.add, op1=ALU.add).then_inc(h_ready, 1)
            dve.wait_ge(hrows_ps, 1)
            for g in range(2):
                part = x_rows[:, 4 * g:4 * g + 4, :]
                last = nc.vector.tensor_tensor(part, R[g][:, :].rearrange("p (t d) -> p t d", d=D), part, ALU.add)
            last.then_inc(x2_ready, 1)
            dve.wait_ge(x2_ready, 1)

            moments(x_rows, 0, B)
            dve.wait_ge(rowsT_ps, 1)
            normalized(10, rows_n, x_rows, 0, B).then_inc(rows_ready, 1)
            dve.wait_ge(rows_ready, 2)
            nc.vector.tensor_tensor(x3b, rows_n, along(bc[:, BC_BO, :]), ALU.add)
            dve.wait_ge(v1_ones, 2)
            for t in range(B):
                dve.wait_ge(v1_ps, t + 1)
                last = nc.vector.tensor_tensor(
                    v1[:, t, :, 0:H * V1].rearrange("p c (h n) -> p c h n", n=V1)[:, :, :, 0:DH1],
                    banks[2 + t % 2][:, 0:2 * D].rearrange("p (c h d) -> p c h d", c=2, d=DH1),
                    bc[:, BC_BVA:BC_BVA + 2, :].rearrange("p c (h d) -> p c h d", d=DH1), ALU.add)
                last.then_inc(v1_rdy, 1)
            dve.wait_ge(rowsT_ps, 2)
            for n in range(8):
                m, g = n // 2, n % 2
                w = (KA, KT, QA, QT)[m]
                cos, sin = (2, 3) if m < 2 else (0, 1)
                t0, t1 = rope_t[2 * g], rope_t[2 * g + 1]
                dve.wait_ge(rope_ps, n + 1)
                as4 = lambda v: v.rearrange("p (b n) -> p b n", n=P)
                nc.vector.scalar_tensor_tensor(out=as4(t0), in0=as4(banks[4 + 2 * g]),
                                               scalar=vcol[:, R_BQA + w:R_BQA + w + 1],
                                               in1=along(rope[:, cos, :], 4), op0=ALU.add, op1=ALU.mult)
                link(nc.vector.scalar_tensor_tensor(out=as4(t1), in0=as4(banks[5 + 2 * g]), scalar=rbcol[:, w:w + 1],
                                                    in1=along(rope[:, sin, :], 4), op0=ALU.add, op1=ALU.mult))
                nc.vector.tensor_tensor(t0, t0, t1, ALU.add).then_inc(rope_sum, 1)
                dve.wait_ge(rope_hi, n + 1)
                if m < 2:
                    hi, lo = k_hl[:, 4 * g:4 * g + 4, 2 * m, :], k_hl[:, 4 * g:4 * g + 4, 2 * m + 1, :]
                    nc.vector.tensor_tensor(lo.bitcast(F32R), as4(t0), hi, ALU.subtract).then_inc(rope_rdy, 1)
                else:
                    hi = q_hl[:, 2 * (m - 2), g * 512:(g + 1) * 512]
                    lo = q_hl[:, 2 * (m - 2) + 1, g * 512:(g + 1) * 512]
                    nc.vector.tensor_tensor(lo.bitcast(F32R), t0, hi, ALU.subtract).then_inc(rope_rdy, 1)

            def spread_q(t, par):
                dve.wait_ge(C.shifted, count(t - 2, 1, 2))
                for kind in (0, 2):
                    last = nc.vector.tensor_tensor(
                        qblk[par][kind].rearrange("p (h n) -> p h n", h=H),
                        q_hl[:, kind, bass.ds(t * P, P)].unsqueeze(1).broadcast_to([P, H, P]),
                        headmask.unsqueeze(2).broadcast_to([P, H, P]), ALU.mult)
                last.then_inc(C.hi_ready, 3)

            def save_z(t):
                dve.wait_ge(C.y_ps, count(t))
                nc.vector.tensor_tensor(z_rows[:, t, :], R[0][:, 0:D], x3b[:, t, :], ALU.add).then_inc(C.y_ready, 1)

            def attend1_vecs(t, par, more):
                if more:
                    spread_q(t + 1, 1 - par)
                    maximum(C, t + 1, 1 - par, 0, 0)
                    maximum(C, t + 1, 1 - par, 1, 1)
                divide(C, t, 0, DH1)
                if more:
                    maximum(C, t + 1, 1 - par, 2, 0)
                    maximum(C, t + 1, 1 - par, 3, 1)
                divide(C, t, 1, DH1)
                if more:
                    max_operand(C, t + 1, 1 - par, 0)
                save_z(t)

            dve.wait_ge(rope_rdy, 8)
            spread_q(0, 0)
            for pair in range(4):
                maximum(C, 0, 0, pair, pair % 2)
            max_operand(C, 0, 0, 0)
            with dve.Fori(0, B // 2 - 1) as i:
                attend1_vecs(2 * i, 0, True)
                attend1_vecs(2 * i + 1, 1, True)
            attend1_vecs(B - 2, 0, True)
            attend1_vecs(B - 1, 1, False)

            dve.wait_ge(C.y_ready, count(B - 1))
            moments(z_rows, 0, B)
            normalized(11, rows_n, z_rows, 0, B).then_inc(rows_ready, 1)
            for g in range(2):
                dve.wait_ge(ff_ps, g + 1)
                part = z_rows[:, 4 * g:4 * g + 4, :]
                link(nc.vector.tensor_tensor(part, banks[4 + g].rearrange("p (t d) -> p t d", d=D),
                                             along(bc[:, BC_BFFN, :], 4), ALU.add))
                last = nc.vector.scalar_tensor_tensor(
                    out=x_rows[:, 4 * g:4 * g + 4, :].rearrange("p t d -> p (t d)"),
                    in0=part.rearrange("p t d -> p (t d)"), scalar=0.0,
                    in1=x_rows[:, 4 * g:4 * g + 4, :].rearrange("p t d -> p (t d)"), op0=ALU.max, op1=ALU.add)
                link(last)

            moments(x_rows, 0, B)
            dve.wait_ge(rowsT_ps, 3)
            link(normalized(12, rows_n, x_rows, 0, B))
            for g in range(2):
                quantize(xq[:, g * 512:(g + 1) * 512], rows_n.rearrange("p b d -> p (b d)")[:, g * 512:(g + 1) * 512],
                         512).then_inc(xq_rdy, 1)
            for g in range(5):
                if g < 4:
                    for t in (2 * g, 2 * g + 1):
                        dve.wait_ge(silu, t + 1)
                        at = (t % 2) * FF
                        last = nc.vector.tensor_tensor(hidden[g % 2][:, at:at + FF], sil[t % 2],
                                                       banks[3 + 2 * (t % 2)][:, 0:FF], ALU.mult)
                        last.then_inc(hid, 1)
                    dve.wait_ge(hid, 2 * g + 2)
                    if g >= 2:
                        dve.wait_ge(hqT_ps, 2 * g - 2)
                    quantize(hq[g % 2], hidden[g % 2], 2 * FF).then_inc(hq_rdy, 1)
                if g >= 1:
                    for t in (2 * g - 2, 2 * g - 1):
                        dve.wait_ge(dn_ps, t + 1)
                        nc.vector.tensor_tensor(x_rows[:, t, :], banks[6 + t % 2][:, 0:D], x_rows[:, t, :], ALU.add)\
                            .then_inc(out_rdy, 1)

        @block.tensor
        def _(pe):
            mm = nc.tensor.matmul
            pe.wait_ge(vchain, 1)
            pe.wait_ge(ld["vec"], 32)
            nc.tensor.transpose(R[0][:, 0:NVEC], vec_rows[:, :], ident[0:NVEC, 0:NVEC])
            nc.tensor.transpose(R[0][:, 32:36], rb_rot[:, :], ident[0:4, 0:4])
            nc.tensor.transpose(R[0][:, 40:40 + B], mask_f[:, :], ident[0:B, 0:B]).then_inc(prep_ps, 1)

            pe.wait_ge(ld["lora"], 32)
            for l in range(NLIN):
                last = nc.tensor.transpose(banks[6 + l // 4][0:RANK, (l % 4) * P:(l % 4 + 1) * P], lb_rows[:, l, :],
                                           ident)
            last.then_inc(prep_ps, 1)
            pe.wait_ge(ld["w1"], 32)
            for m in range(8):
                last = nc.tensor.transpose(banks[2 + m // 4][:, (m % 4) * P:(m % 4 + 1) * P], w1_s[:, m, :], ident)
            last.then_inc(prep_ps, 1)
            pe.wait_ge(prep_v, 2)
            pe.wait_ge(prep_a, 1)
            for l in range(NLIN):
                dst = banks[4 + l // 4][:, (l % 4) * P:(l % 4 + 1) * P]
                mm(dst, w_deq[:, l, :], ident, start=True, stop=False)
                last = mm(dst, la_s[:, l, :], lbT[:, l, :], start=False, stop=True)
            last.then_inc(prep_ps, 1)
            pe.wait_ge(prep_a, 4)

            def transposes(t, par):
                pe.wait_ge(ln_ready, count(t))
                pe.wait_ge(lnT_ready, count(t - 2, 1, 2))
                nc.tensor.transpose(R[par][:, 0:P], cn[:, par, :], ident)
                nc.tensor.transpose(R[par][:, P:2 * P], xl[:, par, :], ident).then_inc(xposed, 1)

            def project(t, par, more):
                pe.wait_ge(lnT_ready, count(t, 0, 2))
                pe.wait_ge(copied, count(t - 1, 0, 3))
                pe.wait_ge(squared, count(t - 1, 0, 3))
                mm(banks[2], cT[par][:, :], wkv_s[:, 0:512], start=True, stop=True).then_inc(projected, 1)
                pe.wait_ge(v_saved, count(t - 1, 0, 2))
                mm(banks[3], cT[par][:, :], wkv_s[:, 512:1024], start=True, stop=True).then_inc(projected, 1)
                if more:
                    transposes(t + 1, 1 - par)
                pe.wait_ge(lnT_ready, count(t, 1, 2))
                pe.wait_ge(copied, count(t - 1, 1, 3))
                pe.wait_ge(squared, count(t - 1, 1, 3))
                mm(banks[4], lT[par][:, :], wq_s[:, :], start=True, stop=True).then_inc(projected, 1)
                pe.wait_ge(copied, count(t - 1, 2, 3))
                pe.wait_ge(squared, count(t - 1, 2, 3))
                mm(banks[5], lT[par][:, :], wkv_s[:, 0:512], start=True, stop=True).then_inc(projected, 1)
                pe.wait_ge(v_saved, count(t - 1, 1, 2))
                mm(banks[6], lT[par][:, :], wkv_s[:, 512:1024], start=True, stop=True).then_inc(projected, 1)

            pe.wait_ge(prep_v, 1)
            transposes(0, 0)
            pe.wait_ge(ld["wkv"], 16)
            pe.wait_ge(ld["wq"], 16)
            with pe.Fori(0, B // 2 - 1) as i:
                project(2 * i, 0, True)
                project(2 * i + 1, 1, True)
            project(B - 2, 0, True)
            project(B - 1, 1, False)

            KIND = (0, 2, 1)

            def qk_transposes(t, par, which):
                if which == 0:
                    pe.wait_ge(A.input_ready, count(t))
                    pe.wait_ge(A.oT_ready, count(t - 2))
                elif which == 1:
                    pe.wait_ge(A.y_ready, count(t - 2))
                else:
                    pe.wait_ge(A.hi_ready, count(t, 0, 3))
                    pe.wait_ge(A.lo_ready, count(t, 0, 3))
                for pair in range(PAIRS):
                    last = nc.tensor.transpose(R[which % 2][:, pair * P:(pair + 1) * P],
                                               qkn[par][:, KIND[which], pair * P:(pair + 1) * P], ident)
                last.then_inc(A.xposed, 1)

            def scores_for_max(t, par, pair):
                bank = 1 - pair % 2
                if pair < 2:
                    pe.wait_ge(A.hi_ready, count(t, 2 - pair, 3) if pair else count(t, 2, 3))
                    pe.wait_ge(A.lo_ready, count(t, 1 if pair == 0 else 2, 3))
                else:
                    pe.wait_ge(A.maxed, count(t, pair - 2, 4))
                mm(R[bank][:, :], row0hot[:, :], maskrow[:, t, :].unsqueeze(1).broadcast_to([P, 2, 2 * P]),
                   start=True, stop=False)
                for e in range(2):
                    last = mm(R[bank][:, e * 256:(e + 1) * 256], qz_hi[par][:, pair, e, :], kT_hi[par][:, pair, :],
                              start=False, stop=(e == 1))
                last.then_inc(A.scored, 1)

            def max_transpose(a, t, par, bank):
                pe.wait_ge(a.maxed, count(t, 3, 4))
                mm(R[bank][0:H, 0:P], negmax[par][:, :], ident_bf[:, :], start=True, stop=True).then_inc(a.maxT, 1)

            def shifted_scores0(t, par, half):
                pe.wait_ge(A.mblk_ready, count(t))
                pe.wait_ge(A.lo_ready, count(t, 2, 3))
                pe.wait_ge(A.expd, count(t - 1, half, 2))
                for g in range(2):
                    bank = S[half][:, g * 512:(g + 1) * 512]
                    mm(bank, grouphot[:, g, :], mblk[par][:, :, :], start=True, stop=False)
                    for pair in (2 * g, 2 * g + 1):
                        dst = S[half][:, pair * 256:(pair + 1) * 256]
                        keys = slice(half * P, (half + 1) * P)
                        mm(dst, kT_hi[par][:, pair, keys], qz_hi[par][:, pair, :, :], start=False, stop=False)
                        mm(dst, kT_hi[par][:, pair, keys], qz_lo[par][:, pair, :, :], start=False, stop=False)
                        last = mm(dst, kT_lo[par][:, pair, keys], qz_hi[par][:, pair, :, :], start=False,
                                  stop=(pair % 2 == 1))
                last.then_inc(A.shifted, 1)

            def mix(a, t, g, v, width):
                pe.wait_ge(a.divided, count(t - 1, g, 2))
                pe.wait_ge(a.expd, count(t, 1, 2))
                for h in range(4 * g, 4 * g + 4):
                    for half in range(2):
                        last = mm(O[g][:, (h % 4) * VN:(h % 4 + 1) * VN], probs[half][:, h, :],
                                  v[:, t, half, h * width:h * width + VN], start=(half == 0), stop=(half == 1))
                last.then_inc(a.mixed, 1)

            def outputs0(t):
                pe.wait_ge(A.divided, count(t, 1, 2))
                for pair in range(PAIRS):
                    last = nc.tensor.transpose(R[0][:, pair * P:(pair + 1) * P], o_rows[:, pair * P:(pair + 1) * P],
                                               ident)
                last.then_inc(A.oT_ps, 1)
                pe.wait_ge(A.oT_ready, count(t))
                for pair in range(PAIRS):
                    last = mm(R[1][:, 0:D], oT[:, pair, :], wo_s[:, pair, :], start=(pair == 0),
                              stop=(pair == PAIRS - 1))
                last.then_inc(A.y_ps, 1)

            def attend0_mms(t, par, more):
                if more:
                    qk_transposes(t + 1, 1 - par, 0)
                shifted_scores0(t, par, 0)
                if more:
                    qk_transposes(t + 1, 1 - par, 1)
                    qk_transposes(t + 1, 1 - par, 2)
                shifted_scores0(t, par, 1)
                if more:
                    scores_for_max(t + 1, 1 - par, 0)
                    scores_for_max(t + 1, 1 - par, 1)
                mix(A, t, 0, v0, V0)
                if more:
                    scores_for_max(t + 1, 1 - par, 2)
                    scores_for_max(t + 1, 1 - par, 3)
                mix(A, t, 1, v0, V0)
                if more:
                    max_transpose(A, t + 1, 1 - par, 1)
                    pe.wait_ge(A.maxed, count(t + 1, 3, 4))
                    pe.wait_ge(A.mblk_ready, count(t + 1))
                outputs0(t)

            for which in range(3):
                qk_transposes(0, 0, which)
            for pair in range(4):
                scores_for_max(0, 0, pair)
            max_transpose(A, 0, 0, 1)
            pe.wait_ge(ld["wo"], 16)
            with pe.Fori(0, B // 2 - 1) as i:
                attend0_mms(2 * i, 0, True)
                attend0_mms(2 * i + 1, 1, True)
            attend0_mms(B - 2, 0, True)
            attend0_mms(B - 1, 1, False)

            def rows_to_T(n):
                pe.wait_ge(rows_ready, n)
                for t in range(B):
                    last = nc.tensor.transpose(R[t // 4][:, (t % 4) * P:(t % 4 + 1) * P], rows_n[:, t, :], ident)
                last.then_inc(rowsT_ps, 1)

            rows_to_T(1)
            pe.wait_ge(rowsT, 1)
            for blk in range(3):
                for g in range(2):
                    n = 2 * blk + g + 1
                    if n > 2:
                        pe.wait_ge(h_ready, n - 2)
                    for t in range(4):
                        last = mm(banks[2 + g][:, t * P:(t + 1) * P], hT[:, (4 * g + t) * P:(4 * g + t + 1) * P],
                                  wffn[:, 2 * blk, :], start=True, stop=True)
                    last.then_inc(up_ps, 1)
                for g in range(2):
                    n = 2 * blk + g + 1
                    pe.wait_ge(up_norm, n)
                    if n > 2:
                        pe.wait_ge(gelu, n - 2)
                    for t in range(4):
                        last = nc.tensor.transpose(banks[4 + g][:, t * P:(t + 1) * P], yn[g][:, t * P:(t + 1) * P],
                                                   ident)
                    last.then_inc(upT_ps, 1)
                for g in range(2):
                    n = 2 * blk + g + 1
                    pe.wait_ge(gelu, n)
                    mm(banks[6 + g], wffn[:, 2 * blk + 1, :], gT[g], start=True, stop=True).then_inc(down_ps, 1)
            pe.wait_ge(h_ready, 6)
            for t in range(B):
                last = nc.tensor.transpose(R[t // 4][:, (t % 4) * P:(t % 4 + 1) * P], hT[:, t * P:(t + 1) * P], ident)
            last.then_inc(hrows_ps, 1)

            pe.wait_ge(x2_ready, 1)
            for t in range(B):
                last = nc.tensor.transpose(R[t // 4][:, (t % 4) * P:(t % 4 + 1) * P], c_rows[:, t, :], ident)
            last.then_inc(ctxT_ps, 1)
            pe.wait_ge(ctxT_rdy, 1)
            for t in range(B):
                if t >= 2:
                    pe.wait_ge(v1_rdy, t - 1)
                mm(banks[2 + t % 2][:, 0:2 * D], ctxT[:, t * P:(t + 1) * P], w1T[:, VA:VT + 1, :], start=True,
                   stop=True).then_inc(v1_ps, 1)
            rows_to_T(2)
            pe.wait_ge(rowsT, 2)
            pe.wait_ge(prep_v, 4)
            for n in range(8):
                m, g = n // 2, n % 2
                w = (KA, KT, QA, QT)[m]
                src = (ctxT if m < 2 else x3T)[:, g * 512:(g + 1) * 512]
                if n >= 2:
                    pe.wait_ge(rope_sum, n - 1)
                mm(banks[4 + 2 * g], w1T[:, w, :], src, start=True, stop=True)
                mm(banks[5 + 2 * g], w1rot[:, w, :], src, start=True, stop=True).then_inc(rope_ps, 1)

            def scores_for_max1(t, par, pair):
                bank = pair % 2
                if pair < 2:
                    pe.wait_ge(C.input_ready, count(t))
                    pe.wait_ge((C.y_ready, C.oT_ready)[pair], count(t - 2))
                else:
                    pe.wait_ge(C.maxed, count(t, pair - 2, 4))
                for e in range(2):
                    for k in range(2):
                        last = mm(R[bank][:, e * 256 + k * P:e * 256 + (k + 1) * P],
                                  q_bf[par][:, k, 2 * pair + e, :], k_bf[:, k, bass.ds(t * P, P)], start=True,
                                  stop=True)
                last.then_inc(C.scored, 1)

            def shifted_scores1(t, par, half):
                pe.wait_ge(C.mblk_ready, count(t))
                pe.wait_ge(C.input_ready2, count(t))
                pe.wait_ge(C.lo_ready, count(t, 2, 3))
                pe.wait_ge(C.expd, count(t - 1, half, 2))
                for g in range(2):
                    bank = S[half][:, g * 512:(g + 1) * 512]
                    cols = slice(g * 512, (g + 1) * 512)
                    k_hi, k_lo = k_st[par][:, 2 * half, :], k_st[par][:, 2 * half + 1, :]
                    q_hi, q_lo = qblk[par][2 * half][:, cols], qblk[par][2 * half + 1][:, cols]
                    mm(bank, grouphot[:, g, :], mblk[par][:, :, :], start=True, stop=False)
                    mm(bank, k_hi, q_hi, start=False, stop=False)
                    mm(bank, k_hi, q_lo, start=False, stop=False)
                    last = mm(bank, k_lo, q_hi, start=False, stop=True)
                last.then_inc(C.shifted, 1)

            def outputs1(t):
                pe.wait_ge(C.divided, count(t, 1, 2))
                nc.tensor.transpose(R[1][:, 0:P], o_rows[:, 0:P], ident).then_inc(C.oT_ps, 1)
                pe.wait_ge(C.oT_ready, count(t))
                mm(R[0][:, 0:D], oT[:, 0, :], w1T[:, WO, :], start=True, stop=True).then_inc(C.y_ps, 1)

            def attend1_mms(t, par, more):
                shifted_scores1(t, par, 0)
                shifted_scores1(t, par, 1)
                if more:
                    scores_for_max1(t + 1, 1 - par, 0)
                    scores_for_max1(t + 1, 1 - par, 1)
                mix(C, t, 0, v1, V1)
                if more:
                    scores_for_max1(t + 1, 1 - par, 2)
                    scores_for_max1(t + 1, 1 - par, 3)
                mix(C, t, 1, v1, V1)
                if more:
                    max_transpose(C, t + 1, 1 - par, 0)
                    pe.wait_ge(C.mblk_ready, count(t + 1))
                outputs1(t)

            pe.wait_ge(rope_rdy, 8)
            for pair in range(4):
                scores_for_max1(0, 0, pair)
            max_transpose(C, 0, 0, 0)
            with pe.Fori(0, B // 2 - 1) as i:
                attend1_mms(2 * i, 0, True)
                attend1_mms(2 * i + 1, 1, True)
            attend1_mms(B - 2, 0, True)
            attend1_mms(B - 1, 1, False)

            rows_to_T(3)
            pe.wait_ge(rowsT, 3)
            for t in range(B):
                last = mm(banks[4 + t // 4][:, (t % 4) * P:(t % 4 + 1) * P], hT[:, t * P:(t + 1) * P], w1T[:, WF, :],
                          start=True, stop=True)
                if t % 4 == 3:
                    last.then_inc(ff_ps, 1)

            pe.wait_ge(w4q_rdy, 1)
            pe.wait_ge(ff_ps, 2)
            pe.wait_ge(xq_rdy, 1)
            for k in range(2):
                for c, width in enumerate(CW):
                    nc.tensor.transpose(banks[2 + k][:, c * P:c * P + width],
                                        w4q[0:width, (3 * k + c) * D:(3 * k + c + 1) * D], ident[0:width, 0:width])
            for c, width in enumerate(CW):
                last = nc.tensor.transpose(banks[4][0:width, c * P:(c + 1) * P],
                                           w4q[:, 768 + c * P:768 + c * P + width], ident)
            last.then_inc(w4T_ps, 1)
            for g in range(2):
                pe.wait_ge(xq_rdy, g + 1)
                for t in range(4):
                    last = nc.tensor.transpose(R[g][:, t * P:(t + 1) * P], xq[:, (4 * g + t) * P:(4 * g + t + 1) * P],
                                               ident)
                last.then_inc(xqT_ps, 1)
            pe.wait_ge(w4T_rdy, 1)

            def gate_up(t):
                if t >= 2:
                    pe.wait_ge(hid, t - 1)
                for k in range(2):
                    last = mm(banks[2 + 2 * (t % 2) + k][:, 0:FF], xqT[t // 4][:, (t % 4) * P:(t % 4 + 1) * P],
                              wguT[:, k, :], start=True, stop=True)
                last.then_inc(gu_ps, 1)

            def down(t):
                pe.wait_ge(hq_rdy, t // 2 + 1)
                if t >= 2:
                    pe.wait_ge(hqT_rdy, t - 1)
                at = (t % 2) * FF
                for c, width in enumerate(CW):
                    last = nc.tensor.transpose(R[t % 2][0:width, c * P:(c + 1) * P],
                                               hq[(t // 2) % 2][:, at + c * P:at + c * P + width], ident)
                last.then_inc(hqT_ps, 1)
                pe.wait_ge(hqT_rdy, t + 1)
                if t >= 2:
                    pe.wait_ge(out_rdy, t - 1)
                for c, width in enumerate(CW):
                    last = mm(banks[6 + t % 2][:, 0:D], hqT[t % 2][0:width, c * P:(c + 1) * P], wdT[0:width, c, :],
                              start=(c == 0), stop=(c == 2))
                last.then_inc(dn_ps, 1)

            pe.wait_ge(xqT_rdy, 1)
            gate_up(0)
            gate_up(1)
            for g in range(1, 5):
                if g < 4:
                    pe.wait_ge(xqT_rdy, 1 + g // 2)
                    gate_up(2 * g)
                    gate_up(2 * g + 1)
                down(2 * g - 2)
                down(2 * g - 1)


def shape_constants():
    c = np.zeros((P, NCONST), np.float32)
    c[:, C_ID:C_ID + P] = np.eye(P, dtype=np.float32)
    half = DH1 // 2
    inv = (1.0 / 10000.0 ** (np.arange(0, DH1, 2, dtype=np.float32) / np.float32(DH1))).astype(np.float32)
    angle = np.arange(P, dtype=np.float32)[None, :] * inv[np.arange(P) % half][:, None]
    cos, sin = np.cos(angle).astype(np.float32), np.sin(angle).astype(np.float32)
    scale = np.float32(1.0 / math.sqrt(DH1))
    for k, a in enumerate((cos * scale, sin * scale, cos, sin)):
        c[:, C_ROPE + k * P:C_ROPE + (k + 1) * P] = a
    for h in range(H):
        c[h * DH1:(h + 1) * DH1, C_HM + h] = 1
        c[h, C_GH + (h // 4) * P:C_GH + (h // 4 + 1) * P] = 1
        c[h, C_M4 + h % 4] = 1
    c[0, C_ROW0:C_ROW0 + P] = 1
    return c


def kernel(**i):
    import numpy as _np
    import concourse.bacc as _bacc
    from concourse import mybir as _mybir
    from concourse.bass_utils import run_bass_kernel_spmd as _run

    a = {k: _np.ascontiguousarray(v) for k, v in i.items()}
    e = EXPERT
    two = lambda v: _np.concatenate([v, v])
    rows = [*a["L0_ffn_biases"], *a["L0_ffn_ln_gamma"], *a["L0_ffn_ln_beta"], a["L0_xattn_ln_x_w"],
            a["L0_xattn_ln_x_b"], a["L0_xattn_ln_l_w"], a["L0_xattn_ln_l_b"], two(a["L0_xattn_q_scale"]),
            two(a["L0_xattn_k_scale"])]
    rows += [a[f"L1_xattn_b_{n}"][e] for n in ("qa", "qt", "ka", "kt")]
    rows += [a["L1_xattn_gamma"][e], a["L1_xattn_beta"][e], a["L0_xattn_ln_o_w"], a["L0_xattn_ln_o_b"]]
    rows += [a[f"L1_xattn_b_{n}"][e] for n in ("va", "vt", "o", "ffn")]
    arrays = {
        "x": a["x"], "ctx": a["ctx_1024"], "mask": a["mask_BxS2_bk0"],
        "wq": a["L0_xattn_Wq"], "wkv": a["L0_xattn_Wkv"], "wo": a["L0_xattn_Wo"],
        "qweights": a["L0_ffn_qweights"], "qscales": a["L0_ffn_scales"], "lora_a": a["L0_ffn_lora_a"],
        "lora_b": a["L0_ffn_lora_b"], "vecs": _np.stack(rows),
        "ropebias": _np.stack([a[f"L1_xattn_b_{n}"][e] for n in ("qa", "qt", "ka", "kt")]),
        "w1": _np.stack([a[f"L1_xattn_W_{n}"][e] for n in ("qa", "qt", "ka", "kt", "va", "vt", "o", "ffn")]),
        "gating": a["L1_xattn_gating_factor"][e:e + 1].reshape(1, 1),
        "w_gate": a["L1_ffn_w_gate"], "w_up": a["L1_ffn_w_up"], "w_down": a["L1_ffn_w_down"],
        "consts": shape_constants(),
    }
    nc = _bacc.Bacc("TRN2", target_bir_lowering=False, num_devices=1)
    aps = [nc.dram_tensor(f"in_{n}", v.shape, _mybir.dt.from_np(v.dtype), kind="ExternalInput").ap()
           for n, v in arrays.items()]
    out = nc.dram_tensor("out_rows", (B, P, D), F32, kind="ExternalOutput").ap()
    build(nc, *aps, out)
    r = _run(nc, [{f"in_{n}": v for n, v in arrays.items()}], core_ids=[0])
    return r.results[0]["out_rows"]
```
